# Optimizing a Trainium2 kernel written in Bass

```python
import numpy as np
import jax
import jax.numpy as jnp

def _softmax(x, axis=-1):
    return jax.nn.softmax(x, axis=axis)

def _gelu(x):
    return jax.nn.gelu(x, approximate=True)

def _silu(x):
    return jax.nn.silu(x)

def _sigmoid(x):
    return jax.nn.sigmoid(x)

def _layernorm(x, axis=-1, eps=1e-05):
    m = jnp.mean(x, axis=axis, keepdims=True)
    v = jnp.var(x, axis=axis, keepdims=True)
    return (x - m) / jnp.sqrt(v + eps)

def _scatter_add(tgt, idx, src, axis=0):
    return tgt.at[idx].add(src)

def _segment_sum(src, seg, n):
    return jax.ops.segment_sum(src, seg, n)
kernel_name = 'mk_recurrent_d1_jaxref_r8_346896'

def setup_inputs(seed: int=0):
    np.random.seed(seed)
    _w = jnp.asarray

    def _L0_attn_setup():
        import jax, jax.numpy as jnp
        import numpy as np
        BATCH, SEQ, D_EMBED, N_HEADS, D_HEAD = (1, 256, 128, 16, 64)
        MASK_VAL = 10000000000.0
        key = jax.random.key(seed)
        ks = jax.random.split(key, 5)
        s = 1.0 / np.sqrt(D_EMBED).astype(np.float32)
        return {'x': jax.random.normal(ks[0], (BATCH, SEQ, D_EMBED), jnp.float32), 'W_Q': jax.random.normal(ks[1], (N_HEADS, D_HEAD, D_EMBED), jnp.float32) * s, 'W_K': jax.random.normal(ks[2], (N_HEADS, D_HEAD, D_EMBED), jnp.float32) * s, 'W_V': jax.random.normal(ks[3], (N_HEADS, D_HEAD, D_EMBED), jnp.float32) * s, 'W_O': jax.random.normal(ks[4], (N_HEADS, D_EMBED, D_HEAD), jnp.float32) * s}
    _L0_attn_in = _L0_attn_setup()

    def _L0_ffn_setup():
        import jax, jax.numpy as jnp
        import numpy as np
        D = 128
        H = 512
        E = 64
        K = 3
        B, S = (2, 256)
        C = 64
        key = jax.random.key(seed)
        ks = jax.random.split(key, 6)
        s = 0.02
        return {'x': jax.random.normal(ks[0], (B, S, D), jnp.float32), 'gate_w': jax.random.normal(ks[1], (D, E), jnp.float32) * s, 'gate_b': jnp.zeros((E,), jnp.float32), 'w1': jax.random.normal(ks[2], (E, D, H), jnp.float32) * s, 'b1': jnp.zeros((E, H), jnp.float32), 'w2': jax.random.normal(ks[3], (E, H, D), jnp.float32) * s, 'b2': jnp.zeros((E, D), jnp.float32)}
    _L0_ffn_in = _L0_ffn_setup()
    _d = {'L0_attn_x': _L0_attn_in['x'], 'L0_attn_W_Q': _L0_attn_in['W_Q'], 'L0_attn_W_K': _L0_attn_in['W_K'], 'L0_attn_W_V': _L0_attn_in['W_V'], 'L0_attn_W_O': _L0_attn_in['W_O'], 'L0_ffn_gate_w': _L0_ffn_in['gate_w'], 'L0_ffn_gate_b': _L0_ffn_in['gate_b'], 'L0_ffn_w1': _L0_ffn_in['w1'], 'L0_ffn_b1': _L0_ffn_in['b1'], 'L0_ffn_w2': _L0_ffn_in['w2'], 'L0_ffn_b2': _L0_ffn_in['b2']}
    _x0 = _d['L0_attn_x']
    _d['L0_attn_x'] = jax.random.normal(jax.random.fold_in(jax.random.key(seed), 1), (2, 1024, 128), dtype=_x0.dtype)
    del _x0
    return _d

def reference(L0_attn_x, L0_attn_W_Q, L0_attn_W_K, L0_attn_W_V, L0_attn_W_O, L0_ffn_gate_w, L0_ffn_gate_b, L0_ffn_w1, L0_ffn_b1, L0_ffn_w2, L0_ffn_b2):

    def _L0_attn_ref(x, W_Q, W_K, W_V, W_O):
        import jax, jax.numpy as jnp
        import numpy as np
        BATCH, SEQ, D_EMBED, N_HEADS, D_HEAD = (1, 256, 128, 16, 64)
        MASK_VAL = 10000000000.0
        q = jnp.einsum('ahe,bce->bach', W_Q, x)
        k = jnp.einsum('ahe,bce->bach', W_K, x)
        v = jnp.einsum('ahe,bce->bach', W_V, x)
        n = x.shape[1]
        scores = jnp.einsum('bach,baCh->bacC', k, q)
        causal = jnp.tril(jnp.ones((n, n), dtype=bool))
        masked = jnp.where(causal, scores, jnp.float32(-MASK_VAL))
        attn = jax.nn.softmax(masked / np.float32(np.sqrt(D_HEAD)), axis=-1)
        z = jnp.einsum('bacC,baCh->bach', attn, v)
        out = jnp.einsum('aeh,bach->bce', W_O, z)
        return out

    def _L0_ffn_ref(x, gate_w, gate_b, w1, b1, w2, b2):
        import jax, jax.numpy as jnp
        import numpy as np
        D = 128
        H = 512
        E = 64
        K = 3
        B, S = (2, 256)
        C = 64
        xf = x.reshape(-1, D)
        T = xf.shape[0]
        logits = xf @ gate_w + gate_b
        top_l, top_i = jax.lax.top_k(logits, K)
        gates = jax.nn.softmax(top_l, axis=-1)
        fe = top_i.reshape(-1)
        fg = gates.reshape(-1)
        tok = jnp.repeat(jnp.arange(T), K)
        oh = jax.nn.one_hot(fe, E, dtype=jnp.int32)
        pos = (jnp.cumsum(oh, axis=0) * oh).sum(-1) - 1
        valid = pos < C
        buf = jnp.zeros((E, C, D), x.dtype).at[fe, pos].set(xf[tok], mode='drop')
        h = jax.nn.gelu(jnp.einsum('ecd,edh->ech', buf, w1) + b1[:, None, :], approximate=False)
        y = jnp.einsum('ech,ehd->ecd', h, w2) + b2[:, None, :]
        rows = y[fe, jnp.minimum(pos, C - 1)] * (fg * valid.astype(x.dtype))[:, None]
        out = jnp.zeros_like(xf).at[tok].add(rows)
        return out.reshape(x.shape)
    x = L0_attn_x
    xn = _layernorm(x, axis=-1)
    s = _L0_attn_ref(xn, L0_attn_W_Q, L0_attn_W_K, L0_attn_W_V, L0_attn_W_O)
    g = _silu(_L0_ffn_ref(xn, L0_ffn_gate_w, L0_ffn_gate_b, L0_ffn_w1, L0_ffn_b1, L0_ffn_w2, L0_ffn_b2))
    x = x + s * g
    return x

_drawn_inputs = setup_inputs


def setup_inputs(seed=0):
    import zlib

    import numpy as np

    out = dict(_drawn_inputs(seed))
    spreads = {'L0_ffn_gate_b': (0.0, 0.7), 'L0_ffn_b1': (0.0, 0.8), 'L0_ffn_b2': (0.0, 0.759)}
    factors = {'L0_attn_W_Q': 5.867,
     'L0_attn_W_K': 5.547,
     'L0_attn_W_V': 4.734,
     'L0_attn_W_O': 4.679,
     'L0_ffn_gate_w': 4.687,
     'L0_ffn_w1': 8.0,
     'L0_ffn_w2': 8.0}
    for name, (base, spread) in spreads.items():
        noise = np.random.default_rng([zlib.crc32(name.encode()), seed]).standard_normal(out[name].shape)
        drawn = base * np.exp(spread * noise) if base else spread * noise
        out[name] = jnp.asarray(drawn.astype(out[name].dtype))
    for name, factor in factors.items():
        out[name] = (out[name] * factor).astype(out[name].dtype)
    return out
```

```python
from contextlib import ExitStack

import concourse.bass as bass
from concourse import mybir

F32 = mybir.dt.float32
F16 = mybir.dt.float16
BF16 = mybir.dt.bfloat16
U32 = mybir.dt.uint32
ALU = mybir.AluOpType
ACT = mybir.ActivationFunctionType
AX_X = mybir.AxisListType.X

P = 128
B, S, D = 2, 1024, 128
HEADS, DH = 16, 64
PAIRS = HEADS // 2
TILES = B * S // P
ROWS = S // P
E, CAP, HID, K = 64, 64, 512, 3
HB = HID // P
EPS = 1e-5
MASKED = 1e10 / 8
SCALE = -1.0 / 8
GRP = 4
W4 = GRP * P
ITEMS = 2 * B * ROWS
MID_FFN, LAST_FFN = 5, 2
LAST = PAIRS - 1
PROLOGUE_USES = 6
PAST_END = 1 << 20
assert MID_FFN * (PAIRS - 2) + LAST_FFN == E // 2


def row_tile(t):
    return t // (2 * ROWS), (t % (2 * ROWS)) // 2, t % 2


def chunk_plan():
    number, n = {}, 0
    for t in range(ITEMS):
        for c in range(row_tile(t)[1] // GRP + 1):
            number[t, c] = n
            n += 1
    return number


def misc_plan(kind):
    at = []
    for b in range(B):
        s = 2 * ROWS * b
        at += [(s + 9, ("rsum", b, 0)), (s + 10, ("pv", b, 0)), (s + 12, ("out", b, 0)),
               (s + 17, ("rsum", b, 1)), (s + 18, ("pv", b, 1)), (s + 20, ("out", b, 1))]
        if b == 0 or kind != "last":
            at += [(s + 3, ("q", 1 - b, 0)), (s + 4, ("q", 1 - b, 1)), (s + 5, ("k", 1 - b, 0)),
                   (s + 6, ("k", 1 - b, 1)), (s + 13, ("v", 1 - b, 0)), (s + 14, ("v", 1 - b, 1))]
    if kind == "mid":
        for e, s in enumerate((0, 7, 11, 23, 27)):
            at += [(s, ("tok", e)), (s + (2 if s != 7 else 1), ("up", e))]
        at += [(35, ("hidT", 0)), (35, ("hidT", 1)), (37, ("down", 0)), (37, ("hidT", 2)),
               (38, ("down", 1)), (38, ("hidT", 3)), (39, ("down", 2)), (39, ("hidT", 4)),
               (40, ("down", 3)), (41, ("down", 4))]
    if kind == "last":
        at += [(0, ("tok", 0)), (1, ("tok", 1)), (2, ("up", 0)), (3, ("up", 1)),
               (7, ("hidT", 0)), (8, ("hidT", 1)), (10, ("down", 0)), (11, ("down", 1))]
    at.sort(key=lambda x: x[0])
    number = {use: n for n, (_, use) in enumerate(at)}
    steps = {}
    for s, use in at:
        steps.setdefault(s, []).append(use)
    return steps, number


STEPS = 42
CHUNK = chunk_plan()
PLAN = {kind: misc_plan(kind) for kind in ("first", "mid", "last")}
CHUNKS = len(CHUNK)
FIRST_USES, MID_USES = (len(PLAN[k][1]) for k in ("first", "mid"))
assert PROLOGUE_USES % 2 == FIRST_USES % 2 == MID_USES % 2 == CHUNKS % 2 == 0
GELU_STEP = {"mid": 34, "last": 4}


def uses_before(p, kind):
    return PROLOGUE_USES // 2 if kind == "first" else (PROLOGUE_USES + FIRST_USES) // 2 + (p - 1) * (MID_USES // 2)


def build(nc, x, wq, wk, wv, wo, gate_w, gate_b, w1, b1, w2, b2, out):
    slots = nc.dram_tensor("slots_dram", [E * CAP, D], F32).ap()
    results = nc.dram_tensor("results_dram", [E * CAP, D], F32).ap()

    x_v = x.rearrange("b (t p) d -> p (b t) d", p=P)
    out_v = out.rearrange("b (t p) d -> p (b t) d", p=P)

    with ExitStack() as ctx:
        def sb(name, shape, dt=F32):
            return ctx.enter_context(nc.sbuf_tensor(name, shape, dt))

        def psum(name, shape, dt=F32):
            return ctx.enter_context(nc.psum_tensor(name, shape, dt))

        def sem(name):
            return ctx.enter_context(nc.semaphore(name))

        ps_s = [psum(f"ps_s{i}", [P, S]) for i in range(2)]
        ps_t = [psum(f"ps_t{i}", [P, W4]) for i in range(2)]
        ps_m = [psum(f"ps_m{i}", [P, W4]) for i in range(2)]

        ident = sb("ident", [P, P])
        ident_b = sb("ident_b", [P, P], BF16)
        mask = sb("mask", [P, P], BF16)
        earlier = sb("earlier", [P, P], BF16)
        ones_b = sb("ones_b", [P, P], BF16)
        iota_e = sb("iota_e", [P, E])
        xn = sb("xn", [P, TILES, D])
        xnT = sb("xnT", [P, B * S])
        s_acc = sb("s_acc", [P, TILES, D])
        w_qkv = sb("w_qkv", [P, 3, P])
        w_o = sb("w_o", [P, D])
        parts = sb("parts", [P, 4, S], F16)
        q_hl = [sb(f"q_hl{b}", [P, 2, S], F16) for b in range(B)]
        k_hh = [sb(f"k_hh{b}", [P, 2, S], F16) for b in range(B)]
        k_ll = [sb(f"k_ll{b}", [P, 2, S], F16) for b in range(B)]
        v_sb = [sb(f"v_sb{b}", [P, ROWS, P]) for b in range(B)]
        probs = sb("probs", [P, 3, S])
        row_min = sb("row_min", [P, 4])
        row_sum = sb("row_sum", [P, B, ROWS, 2, 1])
        row_rec = sb("row_rec", [P, 2, GRP, 2, DH])
        probsT = [sb(f"probsT{g}", [P, 2, GRP * (g + 1), W4]) for g in range(2)]
        rec_rows = sb("rec_rows", [P, 2, W4])
        z_sb = sb("z_sb", [P, 2, W4])
        tok = sb("tok", [P, 3, D])
        w1_sb = sb("w1_sb", [P, 3, 2, HID])
        b1_sb = sb("b1_sb", [P, 3, HID])
        w2_sb = sb("w2_sb", [P, MID_FFN, 2, HB, D])
        b2_sb = sb("b2_sb", [P, MID_FFN, D])
        tokT = sb("tokT", [P, 2, P])
        hid = sb("hid", [P, MID_FFN, HID])
        hidT = sb("hidT", [P, 2, HB, P])
        y_sb = sb("y_sb", [P, MID_FFN, D])
        gathered = sb("gathered", [P, GRP, K, D])
        gate_w_sb = sb("gate_w_sb", [P, E])
        gate_b_sb = sb("gate_b_sb", [P, 1, E])
        rstd = sb("rstd", [P, TILES])
        expert = sb("expert", [P, TILES, K, 1])
        place = sb("place", [P, TILES, K])
        over = sb("over", [P, TILES, K])
        gate = sb("gate", [P, TILES, K])
        gate_sum = sb("gate_sum", [P, TILES, 1])
        to_slot = sb("to_slot", [P, TILES * K], U32)
        from_slot = sb("from_slot", [P, TILES * K], U32)
        g1_flat = probsT[1][:, :, :, :].rearrange("p a b c -> p (a b c)")
        g0_flat = probsT[0][:, :, :, :].rearrange("p a b c -> p (a b c)")
        hot = g1_flat[:, 0:TILES * K * E].rearrange("p (t k e) -> p t k e", t=TILES, k=K)
        hot_pos = g1_flat[:, TILES * K * E:2 * TILES * K * E].rearrange("p (t k e) -> p t k e", t=TILES, k=K)
        logits = g0_flat[:, 0:TILES * E].rearrange("p (t e) -> p t e", t=TILES)
        two_hot = g0_flat[:, TILES * E:2 * TILES * E].rearrange("p (t e) -> p t e", t=TILES)
        chosen = g0_flat[:, 2048:2560].bitcast(BF16).rearrange("p (t e) -> p t e", t=TILES)
        top = g0_flat[:, 2560:2688].rearrange("p (t k) -> p t k", t=TILES)
        top_i = g0_flat[:, 2688:2816].bitcast(U32).rearrange("p (t k) -> p t k", t=TILES)
        stats = g0_flat[:, 2816:2912].rearrange("p (t k) -> p t k", t=TILES)
        mean_var = g0_flat[:, 2912:2944].rearrange("p (t k) -> p t k", t=TILES)
        zeros = w2_sb[:, 0, :, :, :].rearrange("p a b c -> p (a b c)")
        x_sb = s_acc
        x_late = parts[:, :, :].rearrange("p a s -> p (a s)").bitcast(F32).rearrange("p (t d) -> p t d", t=TILES)
        silu = [probsT[0][:, b, :, :].rearrange("p a (c d) -> p (a c) d", d=D)[:, 0:ROWS, :] for b in range(B)]
        f_sum = xn

        x_in = [sem(f"x_in{i}") for i in range(4)]
        gate_in = sem("gate_in")
        var_ready = sem("var_ready")
        std_ready = sem("std_ready")
        xT_ready = sem("xT_ready")
        xT_copied = sem("xT_copied")
        consts = sem("consts")
        acc_zero = sem("acc_zero")
        xn_ready = sem("xn_ready")
        logits_ready = sem("logits_ready")
        logits_read = sem("logits_read")
        chosen_ready = sem("chosen_ready")
        pos_ready = sem("pos_ready")
        pos_read = sem("pos_read")
        gate_diff = sem("gate_diff")
        gate_exp = sem("gate_exp")
        routed = sem("routed")
        zero_set = sem("zero_set")
        zero_filled = sem("zero_filled")
        scattered = sem("scattered")
        dve_chain = sem("dve_chain")
        pool_chain = sem("pool_chain")

        w_in = sem("w_in")
        wo_in = sem("wo_in")
        stacked = [sem(f"stacked{b}") for b in range(B)]
        hi_ready = sem("hi_ready")
        scores_ready = sem("scores_ready")
        min_ready = sem("min_ready")
        exp_ready = sem("exp_ready")
        rec_ready = sem("rec_ready")
        t_ready = sem("t_ready")
        t_done = [sem(f"t_done{i}") for i in range(2)]
        misc_ready = sem("misc_ready")
        misc_done = [sem(f"misc_done{i}") for i in range(2)]
        ffn_in = [sem(f"ffn_in{e}") for e in range(MID_FFN)]
        down_in = [sem(f"down_in{e}") for e in range(MID_FFN)]
        gelu_done = sem("gelu_done")
        y_stored = [sem(f"y_stored{e}") for e in range(MID_FFN)]
        got = [sem(f"got{i}") for i in range(GRP)]
        got_used = sem("got_used")
        x_again = sem("x_again")
        silu_exp = sem("silu_exp")
        result = sem("result")
        stored = sem("stored")

        def misc(p, kind, use):
            n = PLAN[kind][1][use]
            return n % 2, uses_before(p, kind) + n // 2

        def wait_misc_ready(eng, p, kind, use):
            eng.wait_ge(misc_ready, 2 * uses_before(p, kind) + PLAN[kind][1][use] + 1)

        def wait_misc_done(eng, p, kind, use):
            bank, before = misc(p, kind, use)
            eng.wait_ge(misc_done[bank], before + 1)

        def iterations(eng, body):
            body(0, "first")
            with eng.Fori(1, LAST) as p:
                body(p, "mid")
            body(LAST, "last")

        def ffn_count(kind):
            return {"first": 0, "mid": MID_FFN, "last": LAST_FFN}[kind]

        block = ctx.enter_context(nc.Block())

        @block.sync
        def _(sp):
            for i in range(4):
                sp.dma_start(x_sb[:, 4 * i:4 * i + 4, :], x_v[:, 4 * i:4 * i + 4, :]).then_inc(x_in[i], 16)

            def load_heads(pair):
                for i, w in enumerate((wq, wk, wv)):
                    sp.dma_start(w_qkv[:, i, :], w[pair, :, :]).then_inc(w_in, 16)

            def load_wo(pair):
                sp.dma_start(w_o[:, :], wo[pair, :, :]).then_inc(wo_in, 16)

            def stack(b):
                for dst, half, i in ((q_hl, 0, 0), (q_hl, 1, 1), (k_hh, 0, 2), (k_hh, 1, 2), (k_ll, 0, 3),
                                     (k_ll, 1, 3)):
                    for h in range(2):
                        sp.dma_start(dst[b][DH * half:DH * half + DH, h, :],
                                     parts[DH * h:DH * h + DH, i, :]).then_inc(stacked[b], 16)

            def load_up(pair, e):
                sp.dma_start(tok[:, e % 3, :], slots[bass.ds(pair * P, P), :]).then_inc(ffn_in[e], 16)
                sp.dma_start(w1_sb[:, e % 3, :, :],
                             w1[bass.ds(pair * 2, 2), :, :].rearrange("e d h -> d e h")).then_inc(ffn_in[e], 16)
                for i in range(2):
                    sp.dma_start(b1_sb[64 * i:64 * i + 64, e % 3, :],
                                 b1[bass.ds(pair * 2 + i, 1), :].to_broadcast([64, HID])).then_inc(ffn_in[e], 16)

            def load_down(pair, e):
                for i in range(2):
                    sp.dma_start(w2_sb[:, e, i, :, :].rearrange("p a b -> p (a b)"),
                                 w2[bass.ds(pair * 2 + i, 1), :, :].rearrange("e (p t) d -> (e p) (t d)", t=HB)
                                 ).then_inc(down_in[e], 16)
                    sp.dma_start(b2_sb[64 * i:64 * i + 64, e, :],
                                 b2[bass.ds(pair * 2 + i, 1), :].to_broadcast([64, D])).then_inc(down_in[e], 16)

            sp.dma_start(gate_w_sb[:, :], gate_w).then_inc(gate_in, 16)
            sp.dma_start(gate_b_sb[:, 0, :], gate_b.rearrange("(a e) -> a e", a=1).to_broadcast([P, E])
                         ).then_inc(gate_in, 16)
            load_heads(0)
            load_wo(0)
            sp.wait_ge(zero_set, 1)
            for i in range(4):
                sp.dma_start(slots.rearrange("(q p r) d -> q p (r d)", q=4, p=P)[i, :, :], zeros).then_inc(
                    zero_filled, 16)
            for i in range(2):
                sp.wait_ge(misc_done[i], 2)
            stack(0)
            sp.wait_ge(zero_filled, 64)

            def body(p, kind):
                n_ffn = ffn_count(kind)
                first_pair = 0 if kind == "first" else (p - 1) * MID_FFN

                def number(value):
                    return value if isinstance(value, int) else sp.snap(sp.to_reg(value))

                half = uses_before(p, kind)
                all_before = number(half)
                scored_before = number(p * ITEMS)
                scored_half = number(p * ITEMS + ITEMS // 2)
                parts_of = {b: [number(misc(p, kind, ("k", b, i))[1] + 1) for i in range(2)]
                            for b in ((0, 1) if kind != "last" else (1,))}
                ups = [number(misc(p, kind, ("up", e))[1] + 1) for e in range(n_ffn)]
                downs = [number(misc(p, kind, ("down", e))[1] + 1) for e in range(n_ffn)]
                if kind != "last":
                    values_made = number(2 * half + PLAN[kind][1]["v", 1, 1] + 1)
                    outs_made = number(2 * half + PLAN[kind][1]["out", 1, 1] + 1)
                stores_before = number(16 * p)

                def bank(use):
                    return misc_done[PLAN[kind][1][use] % 2]

                if n_ffn:
                    for i in range(2):
                        sp.wait_ge(misc_done[i], all_before)
                    for e in range(n_ffn):
                        load_down(first_pair + e, e)
                if kind == "mid":
                    load_up(first_pair + 2, 2)
                    sp.wait_ge(bank(("up", 0)), ups[0])
                    load_up(first_pair + 3, 3)
                for i in range(2):
                    sp.wait_ge(bank(("k", 1, i)), parts_of[1][i])
                if kind != "first":
                    sp.wait_ge(scores_ready, scored_before)
                stack(1)
                if kind == "mid":
                    sp.wait_ge(bank(("up", 1)), ups[1])
                    load_up(first_pair + 4, 4)
                if kind == "last":
                    sp.wait_ge(stacked[1], 192 * (p + 1))
                    sp.dma_start(x_late, x_v).then_inc(x_again, 16)
                    for e in range(n_ffn):
                        sp.wait_ge(bank(("down", e)), downs[e])
                        store_y(first_pair + e, e)
                    return
                sp.wait_ge(misc_ready, values_made)
                load_heads(p + 1)
                for i in range(2):
                    sp.wait_ge(bank(("k", 0, i)), parts_of[0][i])
                sp.wait_ge(scores_ready, scored_half)
                stack(0)
                if kind == "first":
                    sp.wait_ge(scattered, 16 * TILES * K)
                for e in (0, 1):
                    if kind == "mid":
                        sp.wait_ge(bank(("up", 3 + e)), ups[3 + e])
                    load_up(e if kind == "first" else first_pair + MID_FFN + e, e)
                for e in range(n_ffn):
                    sp.wait_ge(bank(("down", e)), downs[e])
                    store_y(first_pair + e, e)
                for e in range(n_ffn):
                    sp.wait_ge(y_stored[e], stores_before)
                sp.wait_ge(misc_ready, outs_made)
                load_wo(p + 1)

            def store_y(pair, e):
                sp.dma_start(results[bass.ds(pair * P, P), :], y_sb[:, e, :]).then_inc(y_stored[e], 16)

            iterations(sp, body)
            for b in range(B):
                sp.wait_ge(result, b + 1)
                sp.dma_start(out_v[:, ROWS * b:ROWS * b + ROWS, :], silu[b]).then_inc(stored, 16)
            sp.wait_ge(stored, 32)

        @block.gpsimd
        def _(pool):
            def link(n, ins):
                ins.then_inc(pool_chain, 1)
                pool.wait_ge(pool_chain, n)

            pool.memset(ident[:, :], 0.0)
            pool.memset(ident_b[:, :], 0.0)
            pool.memset(mask[:, :], MASKED)
            pool.memset(earlier[:, :], 1.0)
            pool.memset(ones_b[:, :], 1.0)
            link(1, pool.memset(iota_e[:, :], 0.0))
            diagonal = dict(compare_op=ALU.not_equal, fill=1.0, base=0, pattern=[[-1, P]], channel_multiplier=1)
            above = dict(compare_op=ALU.is_gt, fill=0.0, base=0, pattern=[[1, P]], channel_multiplier=-1)
            pool.affine_select(out=ident[:, :], in_=ident[:, :], **diagonal)
            pool.affine_select(out=ident_b[:, :], in_=ident_b[:, :], **diagonal)
            pool.affine_select(out=mask[:, :], in_=mask[:, :], **above)
            pool.affine_select(out=earlier[:, :], in_=earlier[:, :], **above)
            pool.iota(iota_e[:, :], pattern=[[1, E]], base=0, channel_multiplier=0,
                      allow_small_or_imprecise_dtypes=True).then_inc(consts, 1)
            pool.memset(zeros, 0.0).then_inc(zero_set, 1)
            pool.wait_ge(xn_ready, TILES)
            pool.memset(s_acc[:, :, :], 0.0).then_inc(acc_zero, 1)
            pool.wait_ge(zero_filled, 64)
            pool.wait_ge(routed, 1)
            for t in range(TILES):
                for k in range(K):
                    n = t * K + k
                    pool.indirect_dma_start(slots, bass.IndirectOffsetOnAxis(ap=to_slot[:, n:n + 1], axis=0),
                                            xn[:, t, :], None, bounds_check=E * CAP - 1,
                                            oob_is_err=False).then_inc(scattered, 16)
            for e in range(MID_FFN):
                pool.wait_ge(y_stored[e], 16 * (PAIRS - 2 + (e < LAST_FFN)))
            for t in range(TILES):
                if t >= GRP and t % GRP == 0:
                    pool.wait_ge(got_used, t // GRP)
                for k in range(K):
                    n = t * K + k
                    pool.indirect_dma_start(gathered[:, t % GRP, k, :], None, results,
                                            bass.IndirectOffsetOnAxis(ap=from_slot[:, n:n + 1], axis=0),
                                            bounds_check=E * CAP - 1, oob_is_err=False).then_inc(got[t % GRP], 16)

        @block.tensor
        def _(pe):
            pe.wait_ge(consts, 1)
            for t in range(TILES):
                pe.wait_ge(xn_ready, t + 1)
                pe.transpose(ps_s[t // 8][:, P * (t % 8):P * (t % 8) + P], xn[:, t, :], ident[:, :]).then_inc(
                    xT_ready, 1)

            def project(b, what, n, bank):
                at = S * b + W4 * n
                if what != "v":
                    return pe.matmul(ps_m[bank][:, :], w_qkv[:, "qk".index(what), :], xnT[:, at:at + W4],
                                     start=True, stop=True)
                for i in range(GRP):
                    last = pe.matmul(ps_m[bank][:, P * i:P * i + P], xnT[:, at + P * i:at + P * i + P],
                                     w_qkv[:, 2, :], start=True, stop=True)
                return last

            pe.wait_ge(w_in, 48)
            pe.wait_ge(xT_copied, 4)
            for n, (what, i) in enumerate((("q", 0), ("q", 1), ("k", 0), ("k", 1), ("v", 0), ("v", 1))):
                if n >= 2:
                    pe.wait_ge(misc_done[n % 2], n // 2)
                project(0, what, i, n % 2).then_inc(misc_ready, 1)
                if n == 1:
                    pe.wait_ge(gate_in, 32)
                    for t in range(TILES):
                        last = pe.matmul(ps_s[0][:, E * t:E * t + E], xnT[:, P * t:P * t + P], gate_w_sb[:, :],
                                         start=True, stop=True)
                    last.then_inc(logits_ready, 1)
            pe.wait_ge(chosen_ready, 1)
            for t in range(TILES):
                place_t = ps_s[1][:, E * t:E * t + E]
                last = pe.matmul(place_t, earlier[:, :], chosen[:, t, :], start=True, stop=(t == 0))
                for u in range(t):
                    last = pe.matmul(place_t, ones_b[:, :], chosen[:, u, :], start=False, stop=(u == t - 1))
            last.then_inc(pos_ready, 1)
            pe.wait_ge(logits_read, 1)
            pe.wait_ge(pos_read, 1)

            def body(p, kind):
                steps, number = PLAN[kind]
                half = uses_before(p, kind)

                def scores(t):
                    b, i, h = row_tile(t)
                    if t % (ITEMS // 2) == 0:
                        pe.wait_ge(stacked[b], 192 * (p + 1))
                    if kind != "first" or t >= 2:
                        pe.wait_ge(exp_ready, p * ITEMS + t - 1)
                    rows = slice(P * i, P * i + P)
                    n = P * (i + 1)
                    for c in range(0, n, W4):
                        cols = slice(c, min(c + W4, n))
                        o = ps_s[t % 2][:, cols]
                        has_diagonal = cols.stop == n
                        pe.matmul(o, k_hh[b][:, h, rows], q_hl[b][:, h, cols], start=True, stop=False)
                        last = pe.matmul(o, k_ll[b][:, h, rows], q_hl[b][:, h, cols], start=False,
                                         stop=not has_diagonal)
                    last = pe.matmul(ps_s[t % 2][:, P * i:n], ident_b[:, :], mask[:, :], start=False, stop=True)
                    last.then_inc(scores_ready, 1)

                def transposes(t):
                    b, i, h = row_tile(t)
                    pe.wait_ge(exp_ready, p * ITEMS + t + 1)
                    for c in range(i // GRP + 1):
                        n = CHUNK[t, c]
                        if kind != "first" or n >= 2:
                            pe.wait_ge(t_done[n % 2], p * (CHUNKS // 2) + n // 2)
                        for j in range(GRP * c, min(GRP * c + GRP, i + 1)):
                            last = pe.transpose(ps_t[n % 2][:, P * (j % GRP):P * (j % GRP) + P],
                                                probs[:, t % 3, P * j:P * j + P], ident[:, :])
                        last.then_inc(t_ready, 1)

                def misc_use(use):
                    what = use[0]
                    n = number[use]
                    o = ps_m[n % 2]
                    pe.wait_ge(misc_done[n % 2], half + n // 2)
                    if what in "qkv":
                        _, b, i = use
                        pe.wait_ge(w_in, 48 * (p + 1 if b else p + 2))
                        return project(b, what, i, n % 2)
                    if what == "rsum":
                        _, b, g = use
                        pe.wait_ge(rec_ready, 4 * p + 2 * b + g + 1)
                        for i in range(GRP):
                            last = pe.transpose(
                                o[:, P * i:P * i + P],
                                row_rec[:, g, i, :, :].rearrange("p h d -> p (h d)"), ident[:, :])
                        return last
                    if what == "pv":
                        _, b, g = use
                        last_item = 2 * ROWS * b + 8 * g + 7
                        tail = [CHUNK[last_item, c] for c in range(g + 1)] + [CHUNK[last_item - 1, 0]] * (1 - g)
                        for m in tail:
                            pe.wait_ge(t_done[m % 2], p * (CHUNKS // 2) + m // 2 + 1)
                        if b == 0:
                            for i in range(2):
                                pe.wait_ge(misc_done[i], half)
                        else:
                            for i in range(2):
                                wait_misc_done(pe, p, kind, ("v", 1, i))
                        tiles = GRP * (g + 1)
                        for j in range(tiles):
                            off = P * max(0, j - GRP * g)
                            for h in range(2):
                                last = pe.matmul(o[DH * h:DH * h + DH, off:W4], v_sb[b][:, j, DH * h:DH * h + DH],
                                                 probsT[g][:, h, j, off:W4], start=(j == 0), stop=(j == tiles - 1))
                        return last
                    if what == "out":
                        _, b, g = use
                        wait_misc_done(pe, p, kind, ("pv", b, g))
                        pe.wait_ge(wo_in, 16 * (p + 1))
                        for i in range(GRP):
                            last = pe.matmul(o[:, P * i:P * i + P], z_sb[:, g, P * i:P * i + P], w_o[:, :],
                                             start=True, stop=True)
                        return last
                    e = use[1]
                    if what == "tok":
                        pe.wait_ge(ffn_in[e], 64 * p)
                        return pe.transpose(o[:, 0:P], tok[:, e % 3, :], ident[:, :])
                    if what == "up":
                        wait_misc_done(pe, p, kind, ("tok", e))
                        for i in range(2):
                            last = pe.matmul(o[64 * i:64 * i + 64, :], tokT[:, e % 2, 64 * i:64 * i + 64],
                                             w1_sb[:, e % 3, i, :], start=True, stop=True)
                        return last
                    if what == "hidT":
                        pe.wait_ge(gelu_done, (p - 1) * MID_FFN + e + 1)
                        for j in range(HB):
                            last = pe.transpose(o[:, P * j:P * j + P],
                                                hid[:, e, :].rearrange("p (r t) -> p t r", t=HB)[:, j, :], ident[:, :])
                        return last
                    wait_misc_done(pe, p, kind, ("hidT", e))
                    pe.wait_ge(down_in[e], 64 * p)
                    for j in range(HB):
                        for i in range(2):
                            last = pe.matmul(o[64 * i:64 * i + 64, 0:D], hidT[:, e % 2, j, 64 * i:64 * i + 64],
                                             w2_sb[:, e, i, j, :], start=(j == 0), stop=(j == HB - 1))
                    return last

                for s in range(STEPS):
                    if s < ITEMS:
                        scores(s)
                    if 2 <= s < ITEMS + 2:
                        transposes(s - 2)
                    for use in steps.get(s, ()):
                        misc_use(use).then_inc(misc_ready, 1)

            iterations(pe, body)

        @block.scalar
        def _(act):
            act.wait_ge(var_ready, 1)
            act.activation(rstd[:, :], rstd[:, :], ACT.Sqrt).then_inc(std_ready, 1)
            for i in (0, 2):
                act.wait_ge(xT_ready, 4 * i + 4)
                act.activation(xnT[:, W4 * i:W4 * i + W4], ps_s[i // 2][:, (i % 2) * W4:(i % 2) * W4 + W4],
                               ACT.Copy).then_inc(xT_copied, 1)

            def high(what, i, bank):
                act.activation(parts[:, 2 * "qk".index(what), W4 * i:W4 * i + W4], ps_m[bank][:, :], ACT.Copy,
                               scale=(1.0 if what == "q" else SCALE)).then_inc(hi_ready, 1)

            def values(b, i, bank):
                act.activation(v_sb[b][:, GRP * i:GRP * i + GRP, :].rearrange("p a b -> p (a b)"), ps_m[bank][:, :],
                               ACT.Copy).then_inc(misc_done[bank], 1)

            for n, (what, i) in enumerate((("q", 0), ("q", 1), ("k", 0), ("k", 1))):
                act.wait_ge(misc_ready, n + 1)
                high(what, i, n % 2)
            for i in range(2):
                act.wait_ge(misc_ready, 5 + i)
                values(0, i, i)
            act.wait_ge(gate_diff, 1)
            act.activation(gate[:, :, :], gate[:, :, :], ACT.Exp).then_inc(gate_exp, 1)

            def body(p, kind):
                steps, number = PLAN[kind]

                def exponentials(t):
                    b, i, h = row_tile(t)
                    n = P * (i + 1)
                    act.wait_ge(min_ready, p * ITEMS + t + 1)
                    if t >= 3:
                        act.wait_ge(t_ready, p * CHUNKS + CHUNK[t - 3, row_tile(t - 3)[1] // GRP] + 1)
                    elif kind != "first":
                        act.wait_ge(t_ready, p * CHUNKS)
                    act.activation(probs[:, t % 3, 0:n], ps_s[t % 2][:, 0:n], ACT.Exp, bias=row_min[:, t % 4:t % 4 + 1],
                                   scale=-1.0, accum_out=row_sum[:, b, i, h, :]).then_inc(exp_ready, 1)

                def second_chunk(t):
                    b, i, h = row_tile(t)
                    if i < GRP:
                        return
                    n = CHUNK[t, 1]
                    if i == GRP and h == 0:
                        if b == 1:
                            wait_misc_ready(act, p, kind, ("pv", 0, 1))
                        elif kind != "first":
                            act.wait_ge(misc_ready, 2 * uses_before(p, kind))
                    act.wait_ge(t_ready, p * CHUNKS + n + 1)
                    m = i + 1 - GRP
                    act.activation(probsT[1][:, h, GRP:i + 1, P * (i - GRP):P * (i - GRP) + P],
                                   ps_t[n % 2][:, 0:P * m].rearrange("p (a b) -> p a b", b=P),
                                   ACT.Copy).then_inc(t_done[n % 2], 1)

                def consume(use):
                    what = use[0]
                    bank, _ = misc(p, kind, use)
                    if what in "qk":
                        _, b, i = use
                        if what == "q" and i == 0:
                            act.wait_ge(stacked[1 - b], 192 * (p + 1))
                        wait_misc_ready(act, p, kind, use)
                        high(what, i, bank)
                    elif what == "v":
                        _, b, i = use
                        if b == 0:
                            wait_misc_ready(act, p, kind, ("pv", 0, 1))
                        wait_misc_ready(act, p, kind, use)
                        values(b, i, bank)
                    elif what == "rsum":
                        _, b, g = use
                        if b == 1:
                            wait_misc_done(act, p, kind, ("pv", 0, g))
                        elif kind != "first":
                            for i in range(2):
                                act.wait_ge(misc_done[i], uses_before(p, kind))
                        wait_misc_ready(act, p, kind, use)
                        act.activation(rec_rows[:, g, :], ps_m[bank][:, :], ACT.Copy).then_inc(misc_done[bank], 1)
                    elif what == "hidT":
                        e = use[1]
                        if e >= 2:
                            wait_misc_ready(act, p, kind, ("down", e - 2))
                        wait_misc_ready(act, p, kind, use)
                        act.activation(hidT[:, e % 2, :, :].rearrange("p a b -> p (a b)"), ps_m[bank][:, :],
                                       ACT.Copy).then_inc(misc_done[bank], 1)

                for s in range(STEPS):
                    if s < ITEMS:
                        exponentials(s)
                    if 2 <= s < ITEMS + 2:
                        second_chunk(s - 2)
                    if s == GELU_STEP.get(kind):
                        for e in range(ffn_count(kind)):
                            wait_misc_done(act, p, kind, ("up", e))
                            act.activation(hid[:, e, :], hid[:, e, :], ACT.Gelu).then_inc(gelu_done, 1)
                    for use in steps.get(s, ()):
                        consume(use)

            iterations(act, body)
            for b in range(B):
                act.wait_ge(got_used, ROWS // GRP * (b + 1))
                act.activation(silu[b], f_sum[:, ROWS * b:ROWS * b + ROWS, :], ACT.Exp, scale=-1.0).then_inc(silu_exp, 1)

        @block.vector
        def _(dve):
            chain = [0]

            def link(ins):
                chain[0] += 1
                ins.then_inc(dve_chain, 1)
                dve.wait_ge(dve_chain, chain[0])

            for t in range(TILES):
                if t % 4 == 0:
                    dve.wait_ge(x_in[t // 4], 16)
                last = dve.bn_stats(stats[:, t, :], x_sb[:, t, :])
            link(last)
            for t in range(TILES):
                last = dve.bn_aggr(mean_var[:, t, :], stats[:, t, :])
            link(last)
            dve.tensor_scalar(rstd[:, :], mean_var[:, :, 1], EPS, None, ALU.add).then_inc(var_ready, 1)
            dve.wait_ge(std_ready, 1)
            link(dve.reciprocal(rstd[:, :], rstd[:, :]))
            for t in range(TILES):
                dve.tensor_scalar(xn[:, t, :], x_sb[:, t, :], mean_var[:, t, 0:1], rstd[:, t:t + 1], ALU.subtract,
                                  ALU.mult).then_inc(xn_ready, 1)
            for i in (1, 3):
                dve.wait_ge(xT_ready, 4 * i + 4)
                dve.tensor_copy(xnT[:, W4 * i:W4 * i + W4], ps_s[i // 2][:, (i % 2) * W4:(i % 2) * W4 + W4]).then_inc(
                    xT_copied, 1)

            def low(what, i, bank):
                q = 2 * "qk".index(what)
                cols = slice(W4 * i, W4 * i + W4)
                dve.scalar_tensor_tensor(out=parts[:, q + 1, cols], in0=ps_m[bank][:, :],
                                         scalar=(1.0 if what == "q" else SCALE), in1=parts[:, q, cols],
                                         op0=ALU.mult, op1=ALU.subtract).then_inc(misc_done[bank], 1)

            for n, (what, i) in enumerate((("q", 0), ("q", 1), ("k", 0), ("k", 1))):
                dve.wait_ge(hi_ready, n + 1)
                low(what, i, n % 2)

            dve.wait_ge(logits_ready, 1)
            ins = dve.tensor_tensor(logits, ps_s[0][:, :].rearrange("p (t e) -> p t e", t=TILES),
                                    gate_b_sb[:, :, :].to_broadcast([P, TILES, E]), ALU.add)
            ins.then_inc(logits_read, 1)
            dve.wait_ge(logits_read, 1)
            for t in range(TILES):
                last = dve.max(top[:, t, :], logits[:, t, :])
            link(last)
            for t in range(TILES):
                last = dve.max_index(top_i[:, t, :], top[:, t, :], logits[:, t, :])
            link(last)
            link(dve.tensor_copy(expert[:, :, :, 0], top_i[:, :, 0:K]))
            for k in range(K):
                last = dve.tensor_tensor(hot[:, :, k, :], expert[:, :, k, :].to_broadcast([P, TILES, E]),
                                         iota_e[:, :].unsqueeze(1).to_broadcast([P, TILES, E]), ALU.is_equal)
            link(last)
            link(dve.tensor_tensor(two_hot, hot[:, :, 0, :], hot[:, :, 1, :], ALU.add))
            dve.tensor_tensor(chosen[:, :, :], two_hot, hot[:, :, 2, :], ALU.add).then_inc(chosen_ready, 1)
            dve.tensor_tensor(gate[:, :, :], top[:, :, 0:K], top[:, :, 0:1].to_broadcast([P, TILES, K]),
                              ALU.subtract).then_inc(gate_diff, 1)
            dve.wait_ge(gate_exp, 1)
            link(dve.tensor_reduce(gate_sum[:, :, 0], gate[:, :, :], AX_X, ALU.add))
            link(dve.reciprocal(gate_sum[:, :, 0], gate_sum[:, :, 0]))
            link(dve.tensor_tensor(gate[:, :, :], gate[:, :, :], gate_sum[:, :, :].to_broadcast([P, TILES, K]),
                                   ALU.mult))
            dve.wait_ge(pos_ready, 1)
            for k in range(K):
                last = dve.tensor_tensor(hot_pos[:, :, k, :], ps_s[1][:, :].rearrange("p (t e) -> p t e", t=TILES),
                                         hot[:, :, k, :], ALU.mult)
            last.then_inc(pos_read, 1)
            dve.wait_ge(pos_read, 1)
            link(dve.tensor_reduce(place[:, :, :], hot_pos, AX_X, ALU.add))
            link(dve.tensor_scalar(over[:, :, :], place[:, :, :], float(CAP), None, ALU.is_ge))
            kept = hot_pos[:, 0, 0, 0:TILES * K].rearrange("p (t k) -> p t k", k=K)
            slot = hot_pos[:, 1, 0, 0:TILES * K].rearrange("p (t k) -> p t k", k=K)
            link(dve.tensor_scalar(kept, over[:, :, :], -1.0, 1.0, ALU.mult, ALU.add))
            link(dve.tensor_tensor(gate[:, :, :], gate[:, :, :], kept, ALU.mult))
            link(dve.scalar_tensor_tensor(out=slot, in0=expert[:, :, :, 0], scalar=float(CAP), in1=place[:, :, :],
                                          op0=ALU.mult, op1=ALU.add))
            dve.scalar_tensor_tensor(out=to_slot[:, :].rearrange("p (t k) -> p t k", k=K), in0=over[:, :, :],
                                     scalar=float(PAST_END), in1=slot, op0=ALU.mult, op1=ALU.add).then_inc(routed, 1)
            link(dve.tensor_scalar(place[:, :, :], place[:, :, :], float(CAP - 1), None, ALU.min))
            link(dve.scalar_tensor_tensor(out=from_slot[:, :].rearrange("p (t k) -> p t k", k=K),
                                          in0=expert[:, :, :, 0], scalar=float(CAP), in1=place[:, :, :], op0=ALU.mult,
                                          op1=ALU.add))
            dve.wait_ge(acc_zero, 1)

            def gather_sum(q):
                for k in range(K):
                    for i in range(GRP):
                        t = GRP * q + i
                        if k == 0:
                            dve.wait_ge(got[i], 16 * K * (q + 1))
                            last = dve.tensor_scalar(f_sum[:, t, :], gathered[:, i, k, :], gate[:, t, k:k + 1], None,
                                                     ALU.mult)
                        else:
                            last = dve.scalar_tensor_tensor(out=f_sum[:, t, :], in0=gathered[:, i, k, :],
                                                            scalar=gate[:, t, k:k + 1], in1=f_sum[:, t, :],
                                                            op0=ALU.mult, op1=ALU.add)
                    if k == K - 1:
                        last.then_inc(got_used, 1)
                        dve.wait_ge(got_used, q + 1)
                    else:
                        link(last)

            def body(p, kind):
                steps, number = PLAN[kind]

                def minima(t):
                    b, i, h = row_tile(t)
                    dve.wait_ge(scores_ready, p * ITEMS + t + 1)
                    dve.tensor_reduce(row_min[:, t % 4:t % 4 + 1], ps_s[t % 2][:, 0:P * (i + 1)], AX_X,
                                      ALU.min).then_inc(min_ready, 1)

                def first_chunk(t):
                    b, i, h = row_tile(t)
                    g = i // GRP
                    n = CHUNK[t, 0]
                    if i % GRP == 0 and h == 0:
                        if b == 1:
                            wait_misc_ready(dve, p, kind, ("pv", 0, g))
                        elif kind != "first":
                            dve.wait_ge(misc_ready, 2 * uses_before(p, kind))
                    dve.wait_ge(t_ready, p * CHUNKS + n + 1)
                    m = min(i + 1, GRP)
                    dve.tensor_copy(probsT[g][:, h, 0:m, P * (i % GRP):P * (i % GRP) + P],
                                    ps_t[n % 2][:, 0:P * m].rearrange("p (a b) -> p a b", b=P)).then_inc(
                                        t_done[n % 2], 1)

                def reciprocals(b, g):
                    dve.wait_ge(exp_ready, p * ITEMS + 2 * ROWS * b + 8 * g + 8)
                    rows = slice(GRP * g, GRP * g + GRP)
                    dve.reciprocal(row_rec[:, g, :, :, :].rearrange("p i h d -> p (i h) d"),
                                   row_sum[:, b, rows, :, :].rearrange("p i h a -> p (i h) a").to_broadcast(
                                       [P, 2 * GRP, DH])).then_inc(rec_ready, 1)

                def consume(use):
                    what = use[0]
                    bank, _ = misc(p, kind, use)
                    if what in "qk":
                        _, b, i = use
                        unit = 2 * p + 1 if b else 2 * p + 2
                        dve.wait_ge(hi_ready, 4 * unit + 2 * "qk".index(what) + i + 1)
                        low(what, i, bank)
                    elif what == "pv":
                        _, b, g = use
                        wait_misc_done(dve, p, kind, ("rsum", b, g))
                        wait_misc_ready(dve, p, kind, use)
                        dve.tensor_tensor(z_sb[:, g, :], ps_m[bank][:, :], rec_rows[:, g, :], ALU.mult).then_inc(
                            misc_done[bank], 1)
                    elif what == "out":
                        _, b, g = use
                        wait_misc_ready(dve, p, kind, use)
                        t = ROWS * b + GRP * g
                        acc = s_acc[:, t:t + GRP, :].rearrange("p a b -> p (a b)")
                        dve.tensor_tensor(acc, ps_m[bank][:, :], acc, ALU.add).then_inc(misc_done[bank], 1)
                    elif what == "tok":
                        e = use[1]
                        wait_misc_ready(dve, p, kind, use)
                        dve.tensor_copy(tokT[:, e % 2, :], ps_m[bank][:, 0:P]).then_inc(misc_done[bank], 1)
                    elif what == "up":
                        e = use[1]
                        wait_misc_ready(dve, p, kind, use)
                        dve.tensor_tensor(hid[:, e, :], ps_m[bank][:, :], b1_sb[:, e % 3, :], ALU.add).then_inc(
                            misc_done[bank], 1)
                    elif what == "down":
                        e = use[1]
                        wait_misc_ready(dve, p, kind, use)
                        dve.tensor_tensor(y_sb[:, e, :], ps_m[bank][:, 0:D], b2_sb[:, e, :], ALU.add).then_inc(
                            misc_done[bank], 1)

                for s in range(STEPS):
                    if s < ITEMS:
                        minima(s)
                    if 2 <= s < ITEMS + 2:
                        first_chunk(s - 2)
                    if s >= 8 and s % 8 == 0 and s <= ITEMS:
                        reciprocals((s - 8) // 16, (s - 8) // 8 % 2)
                    for use in steps.get(s, ()):
                        consume(use)

            iterations(dve, body)
            for q in range(TILES // GRP):
                gather_sum(q)
            dve.wait_ge(x_again, 16)
            for b in range(B):
                tiles = slice(ROWS * b, ROWS * b + ROWS)
                dve.wait_ge(silu_exp, b + 1)
                link(dve.tensor_scalar(silu[b], silu[b], 1.0, None, ALU.add))
                link(dve.reciprocal(silu[b], silu[b]))
                link(dve.tensor_tensor(silu[b], silu[b], f_sum[:, tiles, :], ALU.mult))
                link(dve.tensor_tensor(silu[b], silu[b], s_acc[:, tiles, :], ALU.mult))
                dve.tensor_tensor(silu[b], silu[b], x_late[:, tiles, :], ALU.add).then_inc(result, 1)


def kernel(L0_attn_x, L0_attn_W_Q, L0_attn_W_K, L0_attn_W_V, L0_attn_W_O, L0_ffn_gate_w, L0_ffn_gate_b, L0_ffn_w1,
           L0_ffn_b1, L0_ffn_w2, L0_ffn_b2):
    import numpy as np
    import concourse.bacc as bacc
    from concourse.bass_utils import run_bass_kernel_spmd

    def by_pair(w):
        return np.ascontiguousarray(np.asarray(w).reshape(PAIRS, 2 * DH, D).transpose(0, 2, 1))

    arrays = {
        "x": np.asarray(L0_attn_x), "wq": by_pair(L0_attn_W_Q), "wk": by_pair(L0_attn_W_K), "wv": by_pair(L0_attn_W_V),
        "wo": np.ascontiguousarray(np.asarray(L0_attn_W_O).transpose(0, 2, 1).reshape(PAIRS, 2 * DH, D)),
        "gate_w": np.asarray(L0_ffn_gate_w), "gate_b": np.asarray(L0_ffn_gate_b),
        "w1": np.asarray(L0_ffn_w1), "b1": np.asarray(L0_ffn_b1), "w2": np.asarray(L0_ffn_w2),
        "b2": np.asarray(L0_ffn_b2),
    }
    nc = bacc.Bacc("TRN2", target_bir_lowering=False, num_devices=1)
    args = [nc.dram_tensor(f"{n}_in", a.shape, mybir.dt.from_np(a.dtype), kind="ExternalInput").ap()
            for n, a in arrays.items()]
    out = nc.dram_tensor("out", [B, S, D], F32, kind="ExternalOutput").ap()
    build(nc, *args, out)
    got = run_bass_kernel_spmd(nc, [{f"{n}_in": a for n, a in arrays.items()}], core_ids=[0])
    return got.results[0]["out"]
```

```python
from contextlib import ExitStack

import concourse.bass as bass
from concourse import mybir

F32 = mybir.dt.float32
F16 = mybir.dt.float16
BF16 = mybir.dt.bfloat16
U32 = mybir.dt.uint32
ALU = mybir.AluOpType
ACT = mybir.ActivationFunctionType
AX_X = mybir.AxisListType.X

P = 128
B, S, D = 2, 1024, 128
HEADS, DH = 16, 64
PAIRS = HEADS // 2
TILES = B * S // P
ROWS = S // P
E, CAP, HID, K = 64, 64, 512, 3
HB = HID // P
EPS = 1e-5
MASKED = 1e10 / 8
SCALE = -1.0 / 8
GRP = 4
W4 = GRP * P
QUARTERS = TILES // GRP
ITEMS = 2 * B * ROWS
MID_FFN, LAST_FFN = 5, 2
LAST = PAIRS - 1
SLOTS = 4
PROLOGUE_USES = 6
PAST_END = 1 << 20
assert MID_FFN * (PAIRS - 2) + LAST_FFN == E // 2 and LAST_FFN == 2


def row_tile(t):
    return t // (2 * ROWS), (t % (2 * ROWS)) // 2, t % 2


def chunk_plan():
    number, n = {}, 0
    for t in range(ITEMS):
        for c in range(row_tile(t)[1] // GRP + 1):
            number[t, c] = n
            n += 1
    return number


MIDDLE = {
    1: [("rsum", 1, 1)], 2: [("pv", 1, 1)], 4: [("out", 1, 1), ("hidT", 0)], 5: [("q", 1, 0), ("q", 1, 1)],
    7: [("down", 0), ("hidT", 1)], 8: [("tok", 0)], 9: [("down", 1), ("hidT", 2)],
    10: [("k", 1, 0), ("k", 1, 1)], 11: [("down", 2), ("hidT", 3)], 12: [("rsum", 0, 0), ("up", 0)],
    13: [("tok", 1), ("v", 1, 0)], 14: [("hidT", 4), ("up", 1)], 15: [("pv", 0, 0), ("v", 1, 1)],
    16: [("tok", 2), ("down", 3)], 17: [("tok", 3), ("rsum", 0, 1)], 18: [("down", 4), ("q", 0, 0)],
    20: [("out", 0, 0), ("q", 0, 1)], 21: [("k", 0, 0)], 22: [("pv", 0, 1)], 24: [("up", 2)],
    25: [("up", 3), ("rsum", 1, 0)], 26: [("k", 0, 1)], 27: [("pv", 1, 0)], 28: [("out", 1, 0), ("tok", 4)],
    29: [("up", 4)], 30: [("v", 0, 0)], 31: [("out", 0, 1), ("v", 0, 1)],
}
FINAL = {
    1: [("tok", 5), ("rsum", 1, 1)], 2: [("pv", 1, 1), ("hidT", 0)],
    4: [("out", 1, 1), ("q", 1, 0), ("q", 1, 1)], 5: [("up", 5), ("hidT", 1)],
    6: [("down", 0), ("k", 1, 0), ("k", 1, 1)], 7: [("hidT", 2)], 8: [("down", 1)],
    9: [("down", 2), ("hidT", 3), ("hidT", 4)], 10: [("tok", 6), ("down", 3), ("up", 6)],
    11: [("down", 4), ("hidT", 5), ("hidT", 6)], 12: [("down", 5), ("down", 6)], 14: [("rsum", 0, 0)],
    15: [("pv", 0, 0)], 18: [("rsum", 0, 1)], 19: [("v", 1, 0)], 20: [("pv", 0, 1)], 21: [("v", 1, 1)],
    23: [("out", 0, 1)], 24: [("out", 0, 0)], 25: [("rsum", 1, 0)], 26: [("pv", 1, 0)], 31: [("out", 1, 0)],
}


def misc_plan(kind):
    def has(use):
        left = use[0] in ("rsum", "pv", "out") and use[1:] == (1, 1)
        return {"first": not left and use[0] not in ("tok", "up", "hidT", "down"),
                "second": use[0] not in ("hidT", "down"), "end": left}.get(kind, True)

    steps = {s: [use for use in uses if has(use)] for s, uses in (FINAL if kind == "last" else MIDDLE).items()}
    number = {use: n for n, use in enumerate(use for s in sorted(steps) for use in steps[s])}
    return steps, number


KINDS = ("first", "second", "mid", "last", "end")
CHUNK = chunk_plan()
PLAN = {kind: misc_plan(kind) for kind in KINDS}
CHUNKS = len(CHUNK)
USES = {kind: len(PLAN[kind][1]) for kind in KINDS}
FIRST_MID = 2
MIDS = LAST - FIRST_MID
BEFORE = {"first": PROLOGUE_USES, "second": PROLOGUE_USES + USES["first"]}
BEFORE["mid"] = BEFORE["second"] + USES["second"]
BEFORE["last"] = BEFORE["mid"] + MIDS * USES["mid"]
BEFORE["end"] = BEFORE["last"] + USES["last"]
assert CHUNKS % 2 == USES["mid"] % 2 == 0
GELUS = {"mid": {2: range(MID_FFN)}, "last": {2: range(MID_FFN), 10: (5, 6)}}
ENDING = {("last", 24): [("sum", 0)], ("end", 0): [("sum", 1)], ("end", 1): [("finish", 0), ("finish", 1), ("sum", 2)], ("end", 2): [("finish", 2), ("sum", 3)], ("end", 4): [("finish", 3)]}


def in_bank(n, bank):
    return (n + 1 - bank) // 2


def build(nc, x, wq, wk, wv, wo, gate_w, gate_b, w1, b1, w2, b2, out):
    slots = nc.dram_tensor("slots_dram", [E * CAP, D], F32).ap()
    results = nc.dram_tensor("results_dram", [E * CAP, D], F32).ap()

    x_v = x.rearrange("b (t p) d -> p (b t) d", p=P)
    out_v = out.rearrange("b (t p) d -> p (b t) d", p=P)

    with ExitStack() as ctx:
        def sb(name, shape, dt=F32):
            return ctx.enter_context(nc.sbuf_tensor(name, shape, dt))

        def psum(name, shape, dt=F32):
            return ctx.enter_context(nc.psum_tensor(name, shape, dt))

        def sem(name):
            return ctx.enter_context(nc.semaphore(name))

        ps_s = [psum(f"ps_s{i}", [P, S]) for i in range(2)]
        ps_t = [psum(f"ps_t{i}", [P, W4]) for i in range(2)]
        ps_m = [psum(f"ps_m{i}", [P, W4]) for i in range(2)]

        ident = sb("ident", [P, P])
        ident_b = sb("ident_b", [P, P], BF16)
        mask = sb("mask", [P, P], BF16)
        earlier = sb("earlier", [P, P], BF16)
        ones_b = sb("ones_b", [P, P], BF16)
        iota_e = sb("iota_e", [P, E])
        xn = sb("xn", [P, TILES, D])
        xnT = sb("xnT", [P, B * S])
        s_acc = sb("s_acc", [P, TILES, D])
        w_qkv = sb("w_qkv", [P, 3, P])
        w_o = sb("w_o", [P, D])
        parts = sb("parts", [P, 4, S], F16)
        q_hl = [sb(f"q_hl{b}", [P, 2, S], F16) for b in range(B)]
        k_hh = [sb(f"k_hh{b}", [P, 2, S], F16) for b in range(B)]
        k_ll = [sb(f"k_ll{b}", [P, 2, S], F16) for b in range(B)]
        v_sb = [sb(f"v_sb{b}", [P, ROWS, P]) for b in range(B)]
        probs = sb("probs", [P, SLOTS, S])
        row_min = sb("row_min", [P, 4])
        row_sum = sb("row_sum", [P, B, ROWS, 2, 1])
        row_rec = sb("row_rec", [P, 2, 2 * GRP, 1])
        rec_wide = sb("rec_wide", [P, 2, 2 * GRP, DH])
        probsT = [sb(f"probsT{g}", [P, 2, GRP * (g + 1), W4]) for g in range(2)]
        rec_rows = sb("rec_rows", [P, 2, W4])
        z_sb = sb("z_sb", [P, 2, W4])
        tok = sb("tok", [P, 3, D])
        w1_sb = sb("w1_sb", [P, 3, 2, HID])
        b1_sb = sb("b1_sb", [P, 3, HID])
        w2_sb = sb("w2_sb", [P, MID_FFN, 2, HB, D])
        b2_sb = sb("b2_sb", [P, MID_FFN, D])
        tokT = sb("tokT", [P, 2, P])
        hid = sb("hid", [P, MID_FFN, HID])
        hidT = sb("hidT", [P, 2, HB, P])
        y_sb = sb("y_sb", [P, MID_FFN, D])
        gate_w_sb = sb("gate_w_sb", [P, E])
        gate_b_sb = sb("gate_b_sb", [P, 1, E])
        rstd = sb("rstd", [P, TILES])
        expert = sb("expert", [P, TILES, K, 1])
        place = sb("place", [P, TILES, K])
        over = sb("over", [P, TILES, K])
        gate = sb("gate", [P, TILES, K])
        gate_sum = sb("gate_sum", [P, TILES, 1])
        to_slot = sb("to_slot", [P, TILES * K], U32)
        from_slot = sb("from_slot", [P, TILES * K], U32)
        g1_flat = probsT[1][:, :, :, :].rearrange("p a b c -> p (a b c)")
        g0_flat = probsT[0][:, :, :, :].rearrange("p a b c -> p (a b c)")
        hot = g1_flat[:, 0:TILES * K * E].rearrange("p (t k e) -> p t k e", t=TILES, k=K)
        hot_pos = g1_flat[:, TILES * K * E:2 * TILES * K * E].rearrange("p (t k e) -> p t k e", t=TILES, k=K)
        logits = g0_flat[:, 0:TILES * E].rearrange("p (t e) -> p t e", t=TILES)
        two_hot = g0_flat[:, TILES * E:2 * TILES * E].rearrange("p (t e) -> p t e", t=TILES)
        chosen = g0_flat[:, 2048:2560].bitcast(BF16).rearrange("p (t e) -> p t e", t=TILES)
        top = g0_flat[:, 2560:2688].rearrange("p (t k) -> p t k", t=TILES)
        top_i = g0_flat[:, 2688:2816].bitcast(U32).rearrange("p (t k) -> p t k", t=TILES)
        stats = g0_flat[:, 2816:2912].rearrange("p (t k) -> p t k", t=TILES)
        mean_var = g0_flat[:, 2912:2944].rearrange("p (t k) -> p t k", t=TILES)
        zeros = w2_sb[:, 0, :, :, :].rearrange("p a b c -> p (a b c)")
        x_sb = s_acc
        x_late = parts[:, :, :].rearrange("p a s -> p (a s)").bitcast(F32).rearrange("p (t d) -> p t d", t=TILES)
        f_sum = xn
        gathered = [whole.rearrange("p (i k d) -> p i k d", k=K, d=D) for whole in (
            w1_sb[:, :, :, :].rearrange("p a b c -> p (a b c)")[:, 0:GRP * K * D],
            w1_sb[:, :, :, :].rearrange("p a b c -> p (a b c)")[:, GRP * K * D:2 * GRP * K * D],
            b1_sb[:, :, :].rearrange("p a b -> p (a b)"),
            w2_sb[:, :, :, :, :].rearrange("p a b c d -> p (a b c d)")[:, 0:GRP * K * D])]

        x_in = [sem(f"x_in{i}") for i in range(4)]
        gate_in = sem("gate_in")
        var_ready = sem("var_ready")
        std_ready = sem("std_ready")
        xT_ready = sem("xT_ready")
        xT_copied = sem("xT_copied")
        consts = sem("consts")
        acc_zero = sem("acc_zero")
        xn_ready = sem("xn_ready")
        logits_ready = sem("logits_ready")
        logits_read = sem("logits_read")
        chosen_ready = sem("chosen_ready")
        pos_ready = sem("pos_ready")
        pos_read = sem("pos_read")
        gate_diff = sem("gate_diff")
        gate_exp = sem("gate_exp")
        routed = sem("routed")
        zero_set = sem("zero_set")
        zero_filled = sem("zero_filled")
        scattered = sem("scattered")
        dve_chain = sem("dve_chain")
        pool_chain = sem("pool_chain")

        w_in = sem("w_in")
        wo_in = sem("wo_in")
        stacked = [sem(f"stacked{b}") for b in range(B)]
        hi_ready = sem("hi_ready")
        scores_ready = sem("scores_ready")
        min_ready = sem("min_ready")
        exp_ready = sem("exp_ready")
        rec_made = sem("rec_made")
        rec_ready = sem("rec_ready")
        t_ready = sem("t_ready")
        t_done = [sem(f"t_done{i}") for i in range(2)]
        misc_ready = sem("misc_ready")
        misc_done = [sem(f"misc_done{i}") for i in range(2)]
        ffn_in = [sem(f"ffn_in{e}") for e in range(MID_FFN)]
        down_in = [sem(f"down_in{e}") for e in range(MID_FFN)]
        gelu_done = sem("gelu_done")
        y_stored = [sem(f"y_stored{e}") for e in range(MID_FFN)]
        got = [sem(f"got{q}") for q in range(QUARTERS)]
        summed = sem("summed")
        x_again = sem("x_again")
        silu_ready = sem("silu_ready")
        result = sem("result")
        stored = sem("stored")

        def misc(p, kind, use):
            n = BEFORE[kind] + PLAN[kind][1][use]
            if kind != "mid":
                return n % 2, n // 2, n
            return n % 2, n // 2 + (p - FIRST_MID) * (USES["mid"] // 2), n + (p - FIRST_MID) * USES["mid"]

        def uses_before(p, kind, bank=None):
            n, m = (BEFORE[kind], USES["mid"]) if bank is None else (in_bank(BEFORE[kind], bank), USES["mid"] // 2)
            return n if kind != "mid" else n + (p - FIRST_MID) * m

        def wait_misc_ready(eng, p, kind, use):
            eng.wait_ge(misc_ready, misc(p, kind, use)[2] + 1)

        def wait_misc_done(eng, p, kind, use):
            bank, before, _ = misc(p, kind, use)
            eng.wait_ge(misc_done[bank], before + 1)

        def iterations(eng, body):
            body(0, "first")
            body(1, "second")
            with eng.Fori(FIRST_MID, LAST) as p:
                body(p, "mid")
            body(LAST, "last")
            body(PAIRS, "end")

        block = ctx.enter_context(nc.Block())

        @block.sync
        def _(sp):
            for i in range(4):
                sp.dma_start(x_sb[:, 4 * i:4 * i + 4, :], x_v[:, 4 * i:4 * i + 4, :]).then_inc(x_in[i], 16)

            def load_heads(pair):
                for i, w in enumerate((wq, wk, wv)):
                    sp.dma_start(w_qkv[:, i, :], w[pair, :, :]).then_inc(w_in, 16)

            def load_wo(pair):
                sp.dma_start(w_o[:, :], wo[pair, :, :]).then_inc(wo_in, 16)

            def stack(b):
                for dst, half, i in ((q_hl, 0, 0), (q_hl, 1, 1), (k_hh, 0, 2), (k_hh, 1, 2), (k_ll, 0, 3),
                                     (k_ll, 1, 3)):
                    for h in range(2):
                        sp.dma_start(dst[b][DH * half:DH * half + DH, h, :],
                                     parts[DH * h:DH * h + DH, i, :]).then_inc(stacked[b], 16)

            def load_up(pair, e):
                sp.dma_start(tok[:, e % 3, :], slots[bass.ds(pair * P, P), :]).then_inc(ffn_in[e], 16)
                sp.dma_start(w1_sb[:, e % 3, :, :],
                             w1[bass.ds(pair * 2, 2), :, :].rearrange("e d h -> d e h")).then_inc(ffn_in[e], 16)
                for i in range(2):
                    sp.dma_start(b1_sb[64 * i:64 * i + 64, e % 3, :],
                                 b1[bass.ds(pair * 2 + i, 1), :].to_broadcast([64, HID])).then_inc(ffn_in[e], 16)

            def load_down(pair, e):
                for i in range(2):
                    sp.dma_start(w2_sb[:, e, i, :, :].rearrange("p a b -> p (a b)"),
                                 w2[bass.ds(pair * 2 + i, 1), :, :].rearrange("e (p t) d -> (e p) (t d)", t=HB)
                                 ).then_inc(down_in[e], 16)
                    sp.dma_start(b2_sb[64 * i:64 * i + 64, e, :],
                                 b2[bass.ds(pair * 2 + i, 1), :].to_broadcast([64, D])).then_inc(down_in[e], 16)

            sp.dma_start(gate_w_sb[:, :], gate_w).then_inc(gate_in, 16)
            sp.dma_start(gate_b_sb[:, 0, :], gate_b.rearrange("(a e) -> a e", a=1).to_broadcast([P, E])
                         ).then_inc(gate_in, 16)
            load_heads(0)
            load_wo(0)
            sp.wait_ge(zero_set, 1)
            for i in range(4):
                sp.dma_start(slots.rearrange("(q p r) d -> q p (r d)", q=4, p=P)[i, :, :], zeros).then_inc(
                    zero_filled, 16)
            for i in range(2):
                sp.wait_ge(misc_done[i], 2)
            stack(0)
            sp.wait_ge(zero_filled, 64)

            def body(p, kind):
                first_pair = (p - 1) * MID_FFN

                def number(value):
                    return value if isinstance(value, int) else sp.snap(sp.to_reg(value))

                def done(use):
                    return misc_done[misc(p, kind, use)[0]], number(misc(p, kind, use)[1] + 1)

                if kind == "end":
                    return
                scored_before = number(p * ITEMS)
                scored_half = number(p * ITEMS + ITEMS // 2)
                k_done = {(b, i): done(("k", b, i)) for b in ((0, 1) if kind != "last" else (1,)) for i in range(2)}
                own = kind in ("second", "mid")
                left = kind in ("mid", "last")
                up_done = [done(("up", e)) for e in range(MID_FFN)] if own else []
                down_done = [done(("down", e)) for e in range(MID_FFN)] if left else []
                if kind != "first":
                    out_made = number(misc(p, kind, ("out", 1, 1))[2] + 1)
                v_made = number(misc(p, kind, ("v", 1, 1))[2] + 1)
                stores = number(16 * (p - 1))

                if kind == "second":
                    sp.wait_ge(scattered, 16 * TILES * K)
                    load_up(0, 0)
                    load_up(1, 1)
                if own:
                    load_up(first_pair + 2, 2)
                if kind != "first":
                    sp.wait_ge(misc_ready, out_made)
                    load_wo(p)
                for i in range(2):
                    sp.wait_ge(*k_done[1, i])
                if kind != "first":
                    sp.wait_ge(scores_ready, scored_before)
                stack(1)

                if kind != "last":
                    if own:
                        sp.wait_ge(*up_done[0])
                        load_up(first_pair + 3, 3)
                    sp.wait_ge(misc_ready, v_made)
                    load_heads(p + 1)
                    if own:
                        sp.wait_ge(*up_done[1])
                        load_up(first_pair + 4, 4)
                for e in range(MID_FFN):
                    if left:
                        sp.wait_ge(*down_done[e])
                        store_y(first_pair - MID_FFN + e, e)
                    if own or left and e < LAST_FFN:
                        load_down(first_pair + e, e)
                if kind == "last":
                    sp.wait_ge(stacked[1], 192 * (p + 1))
                    sp.dma_start(x_late, x_v).then_inc(x_again, 16)
                    for e in range(LAST_FFN):
                        sp.wait_ge(*done(("down", MID_FFN + e)))
                        store_y(first_pair + e, e)
                    return
                for i in range(2):
                    sp.wait_ge(*k_done[0, i])
                sp.wait_ge(scores_ready, scored_half)
                if kind == "mid":
                    for e in range(MID_FFN):
                        sp.wait_ge(y_stored[e], stores)
                stack(0)
                if own:
                    for e in (0, 1):
                        sp.wait_ge(*up_done[3 + e])
                        load_up(first_pair + MID_FFN + e, e)

            def store_y(pair, e):
                sp.dma_start(results[bass.ds(pair * P, P), :], y_sb[:, e, :]).then_inc(y_stored[e], 16)

            iterations(sp, body)
            for q in range(QUARTERS):
                sp.wait_ge(result, q + 1)
                sp.dma_start(out_v[:, GRP * q:GRP * q + GRP, :], f_sum[:, GRP * q:GRP * q + GRP, :]).then_inc(stored, 16)
            sp.wait_ge(stored, 16 * QUARTERS)

        @block.gpsimd
        def _(pool):
            def link(n, ins):
                ins.then_inc(pool_chain, 1)
                pool.wait_ge(pool_chain, n)

            pool.memset(ident[:, :], 0.0)
            pool.memset(ident_b[:, :], 0.0)
            pool.memset(mask[:, :], MASKED)
            pool.memset(earlier[:, :], 1.0)
            pool.memset(ones_b[:, :], 1.0)
            link(1, pool.memset(iota_e[:, :], 0.0))
            diagonal = dict(compare_op=ALU.not_equal, fill=1.0, base=0, pattern=[[-1, P]], channel_multiplier=1)
            above = dict(compare_op=ALU.is_gt, fill=0.0, base=0, pattern=[[1, P]], channel_multiplier=-1)
            pool.affine_select(out=ident[:, :], in_=ident[:, :], **diagonal)
            pool.affine_select(out=ident_b[:, :], in_=ident_b[:, :], **diagonal)
            pool.affine_select(out=mask[:, :], in_=mask[:, :], **above)
            pool.affine_select(out=earlier[:, :], in_=earlier[:, :], **above)
            pool.iota(iota_e[:, :], pattern=[[1, E]], base=0, channel_multiplier=0,
                      allow_small_or_imprecise_dtypes=True).then_inc(consts, 1)
            pool.memset(zeros, 0.0).then_inc(zero_set, 1)
            pool.wait_ge(xn_ready, TILES)
            pool.memset(s_acc[:, :, :], 0.0).then_inc(acc_zero, 1)
            pool.wait_ge(zero_filled, 64)
            pool.wait_ge(routed, 1)
            for t in range(TILES):
                for k in range(K):
                    n = t * K + k
                    pool.indirect_dma_start(slots, bass.IndirectOffsetOnAxis(ap=to_slot[:, n:n + 1], axis=0),
                                            xn[:, t, :], None, bounds_check=E * CAP - 1,
                                            oob_is_err=False).then_inc(scattered, 16)
            for e in range(MID_FFN):
                pool.wait_ge(y_stored[e], 16 * (PAIRS - 2 + (e < LAST_FFN)))
            for t in range(TILES):
                for k in range(K):
                    n = t * K + k
                    pool.indirect_dma_start(gathered[t // GRP][:, t % GRP, k, :], None, results,
                                            bass.IndirectOffsetOnAxis(ap=from_slot[:, n:n + 1], axis=0),
                                            bounds_check=E * CAP - 1, oob_is_err=False).then_inc(got[t // GRP], 16)

        @block.tensor
        def _(pe):
            pe.wait_ge(consts, 1)
            for t in range(TILES):
                pe.wait_ge(xn_ready, t + 1)
                pe.transpose(ps_s[t // 8][:, P * (t % 8):P * (t % 8) + P], xn[:, t, :], ident[:, :]).then_inc(
                    xT_ready, 1)

            def project(b, what, n, bank):
                at = S * b + W4 * n
                if what != "v":
                    return pe.matmul(ps_m[bank][:, :], w_qkv[:, "qk".index(what), :], xnT[:, at:at + W4],
                                     start=True, stop=True)
                for i in range(GRP):
                    last = pe.matmul(ps_m[bank][:, P * i:P * i + P], xnT[:, at + P * i:at + P * i + P],
                                     w_qkv[:, 2, :], start=True, stop=True)
                return last

            pe.wait_ge(w_in, 48)
            pe.wait_ge(xT_copied, 4)
            for n, (what, i) in enumerate((("q", 0), ("q", 1), ("k", 0), ("k", 1), ("v", 0), ("v", 1))):
                if n >= 2:
                    pe.wait_ge(misc_done[n % 2], n // 2)
                project(0, what, i, n % 2).then_inc(misc_ready, 1)
                if n == 1:
                    pe.wait_ge(gate_in, 32)
                    for t in range(TILES):
                        last = pe.matmul(ps_s[0][:, E * t:E * t + E], xnT[:, P * t:P * t + P], gate_w_sb[:, :],
                                         start=True, stop=True)
                    last.then_inc(logits_ready, 1)
            pe.wait_ge(chosen_ready, 1)
            for t in range(TILES):
                place_t = ps_s[1][:, E * t:E * t + E]
                last = pe.matmul(place_t, earlier[:, :], chosen[:, t, :], start=True, stop=(t == 0))
                for u in range(t):
                    last = pe.matmul(place_t, ones_b[:, :], chosen[:, u, :], start=False, stop=(u == t - 1))
            last.then_inc(pos_ready, 1)
            pe.wait_ge(logits_read, 1)
            pe.wait_ge(pos_read, 1)

            def body(p, kind):
                steps = PLAN[kind][0]

                def scores(t):
                    b, i, h = row_tile(t)
                    if t % (ITEMS // 2) == 0:
                        pe.wait_ge(stacked[b], 192 * (p + 1))
                    if kind != "first" or t >= 2:
                        pe.wait_ge(exp_ready, p * ITEMS + t - 1)
                    rows = slice(P * i, P * i + P)
                    n = P * (i + 1)
                    for c in range(0, n, W4):
                        cols = slice(c, min(c + W4, n))
                        o = ps_s[t % 2][:, cols]
                        has_diagonal = cols.stop == n
                        pe.matmul(o, k_hh[b][:, h, rows], q_hl[b][:, h, cols], start=True, stop=False)
                        last = pe.matmul(o, k_ll[b][:, h, rows], q_hl[b][:, h, cols], start=False,
                                         stop=not has_diagonal)
                    last = pe.matmul(ps_s[t % 2][:, P * i:n], ident_b[:, :], mask[:, :], start=False, stop=True)
                    last.then_inc(scores_ready, 1)

                def transposes(p, t):
                    b, i, h = row_tile(t)
                    pe.wait_ge(exp_ready, p * ITEMS + t + 1)
                    for c in range(i // GRP + 1):
                        n = CHUNK[t, c]
                        if not isinstance(p, int) or p or n >= 2:
                            pe.wait_ge(t_done[n % 2], p * (CHUNKS // 2) + n // 2)
                        for j in range(GRP * c, min(GRP * c + GRP, i + 1)):
                            last = pe.transpose(ps_t[n % 2][:, P * (j % GRP):P * (j % GRP) + P],
                                                probs[:, t % SLOTS, P * j:P * j + P], ident[:, :])
                        last.then_inc(t_ready, 1)

                def misc_use(use):
                    what = use[0]
                    bank, before, _ = misc(p, kind, use)
                    o = ps_m[bank]
                    pe.wait_ge(misc_done[bank], before)
                    if what in "qkv":
                        _, b, i = use
                        pe.wait_ge(w_in, 48 * (p + 1 if b else p + 2))
                        return project(b, what, i, bank)
                    if what == "rsum":
                        _, b, g = use
                        pe.wait_ge(rec_ready, 4 * p if b and g else 4 * p + 2 * b + g + 1)
                        for i in range(GRP):
                            last = pe.transpose(
                                o[:, P * i:P * i + P],
                                rec_wide[:, g, 2 * i:2 * i + 2, :].rearrange("p h d -> p (h d)"), ident[:, :])
                        return last
                    if what == "pv":
                        _, b, g = use
                        q = p - 1 if b and g else p
                        last_item = 2 * ROWS * b + 8 * g + 7
                        for m in (CHUNK[last_item, g], CHUNK[last_item, g] - 1):
                            pe.wait_ge(t_done[m % 2], q * (CHUNKS // 2) + m // 2 + 1)
                        for i in range(2):
                            if b == 1 and g == 0:
                                wait_misc_done(pe, p, kind, ("v", 1, i))
                            else:
                                pe.wait_ge(misc_done[i], uses_before(p, kind, i))
                        tiles = GRP * (g + 1)
                        for j in range(tiles):
                            off = P * max(0, j - GRP * g)
                            for h in range(2):
                                last = pe.matmul(o[DH * h:DH * h + DH, off:W4], v_sb[b][:, j, DH * h:DH * h + DH],
                                                 probsT[g][:, h, j, off:W4], start=(j == 0), stop=(j == tiles - 1))
                        return last
                    if what == "out":
                        _, b, g = use
                        wait_misc_done(pe, p, kind, ("pv", b, g))
                        pe.wait_ge(wo_in, 16 * p if b and g else 16 * (p + 1))
                        for i in range(GRP):
                            last = pe.matmul(o[:, P * i:P * i + P], z_sb[:, g, P * i:P * i + P], w_o[:, :],
                                             start=True, stop=True)
                        return last
                    e = use[1]
                    e, own = e % MID_FFN, e
                    if what == "tok":
                        pe.wait_ge(ffn_in[e], 64 * p)
                        return pe.transpose(o[:, 0:P], tok[:, e % 3, :], ident[:, :])
                    if what == "up":
                        wait_misc_done(pe, p, kind, ("tok", own))
                        for i in range(2):
                            last = pe.matmul(o[64 * i:64 * i + 64, :], tokT[:, e % 2, 64 * i:64 * i + 64],
                                             w1_sb[:, e % 3, i, :], start=True, stop=True)
                        return last
                    if what == "hidT":
                        pe.wait_ge(gelu_done, (p - 2) * MID_FFN + own + 1)
                        for j in range(HB):
                            last = pe.transpose(o[:, P * j:P * j + P],
                                                hid[:, e, :].rearrange("p (r t) -> p t r", t=HB)[:, j, :], ident[:, :])
                        return last
                    wait_misc_done(pe, p, kind, ("hidT", own))
                    pe.wait_ge(down_in[e], 64 * (p - 1) if own < MID_FFN else 64 * p)
                    for j in range(HB):
                        for i in range(2):
                            last = pe.matmul(o[64 * i:64 * i + 64, 0:D], hidT[:, own % 2, j, 64 * i:64 * i + 64],
                                             w2_sb[:, e, i, j, :], start=(j == 0), stop=(j == HB - 1))
                    return last

                for s in range(ITEMS):
                    if kind != "end":
                        scores(s)
                    if s < 2 and kind != "first":
                        transposes(p - 1, ITEMS - 2 + s)
                    if s >= 2 and kind != "end":
                        transposes(p, s - 2)
                    for use in steps.get(s, ()):
                        misc_use(use).then_inc(misc_ready, 1)

            iterations(pe, body)

        @block.scalar
        def _(act):
            act.wait_ge(var_ready, 1)
            act.activation(rstd[:, :], rstd[:, :], ACT.Sqrt).then_inc(std_ready, 1)
            for i in (0, 2):
                act.wait_ge(xT_ready, 4 * i + 4)
                act.activation(xnT[:, W4 * i:W4 * i + W4], ps_s[i // 2][:, (i % 2) * W4:(i % 2) * W4 + W4],
                               ACT.Copy).then_inc(xT_copied, 1)

            def high(what, i, bank):
                act.activation(parts[:, 2 * "qk".index(what), W4 * i:W4 * i + W4], ps_m[bank][:, :], ACT.Copy,
                               scale=(1.0 if what == "q" else SCALE)).then_inc(hi_ready, 1)

            def values(b, i, bank):
                act.activation(v_sb[b][:, GRP * i:GRP * i + GRP, :].rearrange("p a b -> p (a b)"), ps_m[bank][:, :],
                               ACT.Copy).then_inc(misc_done[bank], 1)

            for n, (what, i) in enumerate((("q", 0), ("q", 1), ("k", 0), ("k", 1))):
                act.wait_ge(misc_ready, n + 1)
                high(what, i, n % 2)
            for i in range(2):
                act.wait_ge(misc_ready, 5 + i)
                values(0, i, i)
            act.wait_ge(gate_diff, 1)
            act.activation(gate[:, :, :], gate[:, :, :], ACT.Exp).then_inc(gate_exp, 1)

            def body(p, kind):
                steps = PLAN[kind][0]

                def exponentials(t):
                    b, i, h = row_tile(t)
                    n = P * (i + 1)
                    act.wait_ge(min_ready, p * ITEMS + t + 1)
                    if t >= SLOTS:
                        act.wait_ge(t_ready, p * CHUNKS + CHUNK[t - SLOTS, row_tile(t - SLOTS)[1] // GRP] + 1)
                    elif kind != "first":
                        u = ITEMS + t - SLOTS
                        act.wait_ge(t_ready, (p - 1) * CHUNKS + CHUNK[u, 1] + 1)
                    act.activation(probs[:, t % SLOTS, 0:n], ps_s[t % 2][:, 0:n], ACT.Exp,
                                   bias=row_min[:, t % 4:t % 4 + 1], scale=-1.0,
                                   accum_out=row_sum[:, b, i, h, :]).then_inc(exp_ready, 1)

                def chunk(p, t):
                    b, i, h = row_tile(t)
                    g = i // GRP
                    n = CHUNK[t, g]
                    if i % GRP == 0 and h == 0:
                        if b == 1:
                            wait_misc_ready(act, p, kind, ("pv", 0, g))
                        elif kind != "first":
                            if g == 1:
                                wait_misc_ready(act, p, kind, ("pv", 1, 1))
                            else:
                                act.wait_ge(misc_ready, uses_before(p, kind))
                    act.wait_ge(t_ready, p * CHUNKS + n + 1)
                    m = i % GRP + 1
                    act.activation(probsT[g][:, h, GRP * g:i + 1, P * (i % GRP):P * (i % GRP) + P],
                                   ps_t[n % 2][:, 0:P * m].rearrange("p (a b) -> p a b", b=P),
                                   ACT.Copy).then_inc(t_done[n % 2], 1)

                def widen(p, b, g):
                    act.wait_ge(rec_made, 4 * p + 2 * b + g + 1)
                    act.activation(rec_wide[:, g, :, :], row_rec[:, g, :, :].to_broadcast([P, 2 * GRP, DH]),
                                   ACT.Copy).then_inc(rec_ready, 1)

                def consume(use):
                    what = use[0]
                    bank = misc(p, kind, use)[0]
                    if what in "qk":
                        _, b, i = use
                        if what == "q" and i == 0:
                            act.wait_ge(stacked[1 - b], 192 * (p + 1))
                        wait_misc_ready(act, p, kind, use)
                        high(what, i, bank)
                    elif what == "v":
                        _, b, i = use
                        if b == 0 or kind != "first":
                            wait_misc_ready(act, p, kind, ("pv", b, 1))
                        wait_misc_ready(act, p, kind, use)
                        values(b, i, bank)
                    elif what == "rsum":
                        _, b, g = use
                        if (b, g) == (1, 0):
                            wait_misc_done(act, p, kind, ("pv", 0, 0))
                        elif (b, g) == (0, 1) and kind != "first":
                            wait_misc_done(act, p, kind, ("pv", 1, 1))
                        elif kind != "first":
                            for i in range(2):
                                act.wait_ge(misc_done[i], uses_before(p, kind, i))
                        wait_misc_ready(act, p, kind, use)
                        act.activation(rec_rows[:, g, :], ps_m[bank][:, :], ACT.Copy).then_inc(misc_done[bank], 1)
                    elif what == "hidT":
                        e = use[1]
                        if e >= 2:
                            wait_misc_ready(act, p, kind, ("down", e - 2))
                        wait_misc_ready(act, p, kind, use)
                        act.activation(hidT[:, e % 2, :, :].rearrange("p a b -> p (a b)"), ps_m[bank][:, :],
                                       ACT.Copy).then_inc(misc_done[bank], 1)

                for s in range(ITEMS):
                    if kind != "end":
                        exponentials(s)
                    if s < 2 and kind != "first":
                        chunk(p - 1, ITEMS - 2 + s)
                    if s >= 2 and kind != "end":
                        chunk(p, s - 2)
                    if s == 0 and kind != "first":
                        widen(p - 1, 1, 1)
                    if s and s % 8 == 0 and kind != "end":
                        widen(p, (s - 8) // 16, (s - 8) // 8 % 2)
                    for e in GELUS.get(kind, {}).get(s, ()):
                        if e < MID_FFN:
                            for i in range(2):
                                act.wait_ge(misc_done[i], uses_before(p, kind, i))
                        else:
                            wait_misc_done(act, p, kind, ("up", e))
                        x_e = hid[:, e % MID_FFN, :]
                        act.activation(x_e, x_e, ACT.Gelu).then_inc(gelu_done, 1)
                    for use in steps.get(s, ()):
                        consume(use)

            iterations(act, body)
            for q in range(QUARTERS):
                act.wait_ge(summed, q + 1)
                act.activation(f_sum[:, GRP * q:GRP * q + GRP, :], f_sum[:, GRP * q:GRP * q + GRP, :],
                               ACT.Silu).then_inc(silu_ready, 1)

        @block.vector
        def _(dve):
            chain = [0]

            def link(ins):
                chain[0] += 1
                ins.then_inc(dve_chain, 1)
                dve.wait_ge(dve_chain, chain[0])

            for t in range(TILES):
                if t % 4 == 0:
                    dve.wait_ge(x_in[t // 4], 16)
                last = dve.bn_stats(stats[:, t, :], x_sb[:, t, :])
            link(last)
            for t in range(TILES):
                last = dve.bn_aggr(mean_var[:, t, :], stats[:, t, :])
            link(last)
            dve.tensor_scalar(rstd[:, :], mean_var[:, :, 1], EPS, None, ALU.add).then_inc(var_ready, 1)
            dve.wait_ge(std_ready, 1)
            link(dve.reciprocal(rstd[:, :], rstd[:, :]))
            for t in range(TILES):
                dve.tensor_scalar(xn[:, t, :], x_sb[:, t, :], mean_var[:, t, 0:1], rstd[:, t:t + 1], ALU.subtract,
                                  ALU.mult).then_inc(xn_ready, 1)
            for i in (1, 3):
                dve.wait_ge(xT_ready, 4 * i + 4)
                dve.tensor_copy(xnT[:, W4 * i:W4 * i + W4], ps_s[i // 2][:, (i % 2) * W4:(i % 2) * W4 + W4]).then_inc(
                    xT_copied, 1)

            def low(what, i, bank):
                q = 2 * "qk".index(what)
                cols = slice(W4 * i, W4 * i + W4)
                dve.scalar_tensor_tensor(out=parts[:, q + 1, cols], in0=ps_m[bank][:, :],
                                         scalar=(1.0 if what == "q" else SCALE), in1=parts[:, q, cols],
                                         op0=ALU.mult, op1=ALU.subtract).then_inc(misc_done[bank], 1)

            for n, (what, i) in enumerate((("q", 0), ("q", 1), ("k", 0), ("k", 1))):
                dve.wait_ge(hi_ready, n + 1)
                low(what, i, n % 2)

            dve.wait_ge(logits_ready, 1)
            ins = dve.tensor_tensor(logits, ps_s[0][:, :].rearrange("p (t e) -> p t e", t=TILES),
                                    gate_b_sb[:, :, :].to_broadcast([P, TILES, E]), ALU.add)
            ins.then_inc(logits_read, 1)
            dve.wait_ge(logits_read, 1)
            for t in range(TILES):
                last = dve.max(top[:, t, :], logits[:, t, :])
            link(last)
            for t in range(TILES):
                last = dve.max_index(top_i[:, t, :], top[:, t, :], logits[:, t, :])
            link(last)
            link(dve.tensor_copy(expert[:, :, :, 0], top_i[:, :, 0:K]))
            for k in range(K):
                last = dve.tensor_tensor(hot[:, :, k, :], expert[:, :, k, :].to_broadcast([P, TILES, E]),
                                         iota_e[:, :].unsqueeze(1).to_broadcast([P, TILES, E]), ALU.is_equal)
            link(last)
            link(dve.tensor_tensor(two_hot, hot[:, :, 0, :], hot[:, :, 1, :], ALU.add))
            dve.tensor_tensor(chosen[:, :, :], two_hot, hot[:, :, 2, :], ALU.add).then_inc(chosen_ready, 1)
            dve.tensor_tensor(gate[:, :, :], top[:, :, 0:K], top[:, :, 0:1].to_broadcast([P, TILES, K]),
                              ALU.subtract).then_inc(gate_diff, 1)
            dve.wait_ge(gate_exp, 1)
            link(dve.tensor_reduce(gate_sum[:, :, 0], gate[:, :, :], AX_X, ALU.add))
            link(dve.reciprocal(gate_sum[:, :, 0], gate_sum[:, :, 0]))
            link(dve.tensor_tensor(gate[:, :, :], gate[:, :, :], gate_sum[:, :, :].to_broadcast([P, TILES, K]),
                                   ALU.mult))
            dve.wait_ge(pos_ready, 1)
            for k in range(K):
                last = dve.tensor_tensor(hot_pos[:, :, k, :], ps_s[1][:, :].rearrange("p (t e) -> p t e", t=TILES),
                                         hot[:, :, k, :], ALU.mult)
            last.then_inc(pos_read, 1)
            dve.wait_ge(pos_read, 1)
            link(dve.tensor_reduce(place[:, :, :], hot_pos, AX_X, ALU.add))
            link(dve.tensor_scalar(over[:, :, :], place[:, :, :], float(CAP), None, ALU.is_ge))
            kept = hot_pos[:, 0, 0, 0:TILES * K].rearrange("p (t k) -> p t k", k=K)
            slot = hot_pos[:, 1, 0, 0:TILES * K].rearrange("p (t k) -> p t k", k=K)
            link(dve.tensor_scalar(kept, over[:, :, :], -1.0, 1.0, ALU.mult, ALU.add))
            link(dve.tensor_tensor(gate[:, :, :], gate[:, :, :], kept, ALU.mult))
            link(dve.scalar_tensor_tensor(out=slot, in0=expert[:, :, :, 0], scalar=float(CAP), in1=place[:, :, :],
                                          op0=ALU.mult, op1=ALU.add))
            dve.scalar_tensor_tensor(out=to_slot[:, :].rearrange("p (t k) -> p t k", k=K), in0=over[:, :, :],
                                     scalar=float(PAST_END), in1=slot, op0=ALU.mult, op1=ALU.add).then_inc(routed, 1)
            link(dve.tensor_scalar(place[:, :, :], place[:, :, :], float(CAP - 1), None, ALU.min))
            link(dve.scalar_tensor_tensor(out=from_slot[:, :].rearrange("p (t k) -> p t k", k=K),
                                          in0=expert[:, :, :, 0], scalar=float(CAP), in1=place[:, :, :], op0=ALU.mult,
                                          op1=ALU.add))
            dve.wait_ge(acc_zero, 1)

            def gather_sum(q):
                dve.wait_ge(got[q], 16 * K * GRP)
                for k in range(K):
                    for i in range(GRP):
                        t = GRP * q + i
                        if k == 0:
                            last = dve.tensor_scalar(f_sum[:, t, :], gathered[q][:, i, k, :], gate[:, t, k:k + 1],
                                                     None, ALU.mult)
                        else:
                            last = dve.scalar_tensor_tensor(out=f_sum[:, t, :], in0=gathered[q][:, i, k, :],
                                                            scalar=gate[:, t, k:k + 1], in1=f_sum[:, t, :],
                                                            op0=ALU.mult, op1=ALU.add)
                    if k == K - 1:
                        last.then_inc(summed, 1)
                    else:
                        link(last)

            def finish(q):
                tiles = slice(GRP * q, GRP * q + GRP)
                dve.wait_ge(silu_ready, q + 1)
                kind, p = ("end", PAIRS) if q == QUARTERS - 1 else ("last", LAST)
                wait_misc_done(dve, p, kind, ("out", q // 2, q % 2))
                link(dve.tensor_tensor(f_sum[:, tiles, :], f_sum[:, tiles, :], s_acc[:, tiles, :], ALU.mult))
                if q == 0:
                    dve.wait_ge(x_again, 16)
                dve.tensor_tensor(f_sum[:, tiles, :], f_sum[:, tiles, :], x_late[:, tiles, :], ALU.add).then_inc(
                    result, 1)

            def body(p, kind):
                steps = PLAN[kind][0]

                def minima(t):
                    b, i, h = row_tile(t)
                    dve.wait_ge(scores_ready, p * ITEMS + t + 1)
                    dve.tensor_reduce(row_min[:, t % 4:t % 4 + 1], ps_s[t % 2][:, 0:P * (i + 1)], AX_X,
                                      ALU.min).then_inc(min_ready, 1)

                def first_chunk(p, t):
                    b, i, h = row_tile(t)
                    if i < GRP:
                        return
                    n = CHUNK[t, 0]
                    if i == GRP and h == 0:
                        if b == 1:
                            wait_misc_ready(dve, p, kind, ("pv", 0, 1))
                        elif kind != "first":
                            wait_misc_ready(dve, p, kind, ("pv", 1, 1))
                    dve.wait_ge(t_ready, p * CHUNKS + n + 1)
                    dve.tensor_copy(probsT[1][:, h, 0:GRP, P * (i % GRP):P * (i % GRP) + P],
                                    ps_t[n % 2][:, :].rearrange("p (a b) -> p a b", b=P)).then_inc(t_done[n % 2], 1)

                def reciprocals(p, b, g):
                    dve.wait_ge(exp_ready, p * ITEMS + 2 * ROWS * b + 8 * g + 8)
                    rows = slice(GRP * g, GRP * g + GRP)
                    dve.reciprocal(row_rec[:, g, :, 0], row_sum[:, b, rows, :, 0].rearrange("p i h -> p (i h)")
                                   ).then_inc(rec_made, 1)

                def consume(use):
                    what = use[0]
                    bank = misc(p, kind, use)[0]
                    if what in "qk":
                        _, b, i = use
                        unit = 2 * p + 1 if b else 2 * p + 2
                        dve.wait_ge(hi_ready, 4 * unit + 2 * "qk".index(what) + i + 1)
                        low(what, i, bank)
                    elif what == "pv":
                        _, b, g = use
                        wait_misc_done(dve, p, kind, ("rsum", b, g))
                        wait_misc_ready(dve, p, kind, use)
                        dve.tensor_tensor(z_sb[:, g, :], ps_m[bank][:, :], rec_rows[:, g, :], ALU.mult).then_inc(
                            misc_done[bank], 1)
                    elif what == "out":
                        _, b, g = use
                        wait_misc_ready(dve, p, kind, use)
                        t = ROWS * b + GRP * g
                        acc = s_acc[:, t:t + GRP, :].rearrange("p a b -> p (a b)")
                        dve.tensor_tensor(acc, ps_m[bank][:, :], acc, ALU.add).then_inc(misc_done[bank], 1)
                    elif what == "tok":
                        e = use[1] % MID_FFN
                        wait_misc_ready(dve, p, kind, use)
                        dve.tensor_copy(tokT[:, e % 2, :], ps_m[bank][:, 0:P]).then_inc(misc_done[bank], 1)
                    elif what == "up":
                        e = use[1] % MID_FFN
                        wait_misc_ready(dve, p, kind, use)
                        dve.tensor_tensor(hid[:, e, :], ps_m[bank][:, :], b1_sb[:, e % 3, :], ALU.add).then_inc(
                            misc_done[bank], 1)
                    elif what == "down":
                        e = use[1] % MID_FFN
                        if use[1] >= MID_FFN:
                            dve.wait_ge(y_stored[e], 16 * (PAIRS - 2))
                        wait_misc_ready(dve, p, kind, use)
                        dve.tensor_tensor(y_sb[:, e, :], ps_m[bank][:, 0:D], b2_sb[:, e, :], ALU.add).then_inc(
                            misc_done[bank], 1)

                for s in range(ITEMS):
                    if kind != "end":
                        minima(s)
                    if s < 2 and kind != "first":
                        first_chunk(p - 1, ITEMS - 2 + s)
                    if s >= 2 and kind != "end":
                        first_chunk(p, s - 2)
                    if s == 0 and kind != "first":
                        reciprocals(p - 1, 1, 1)
                    if s and s % 8 == 0 and kind != "end":
                        reciprocals(p, (s - 8) // 16, (s - 8) // 8 % 2)
                    for use in steps.get(s, ()):
                        consume(use)
                    for what, q in ENDING.get((kind, s), ()):
                        (gather_sum if what == "sum" else finish)(q)

            iterations(dve, body)


def kernel(L0_attn_x, L0_attn_W_Q, L0_attn_W_K, L0_attn_W_V, L0_attn_W_O, L0_ffn_gate_w, L0_ffn_gate_b, L0_ffn_w1,
           L0_ffn_b1, L0_ffn_w2, L0_ffn_b2):
    import numpy as np
    import concourse.bacc as bacc
    from concourse.bass_utils import run_bass_kernel_spmd

    def by_pair(w):
        return np.ascontiguousarray(np.asarray(w).reshape(PAIRS, 2 * DH, D).transpose(0, 2, 1))

    arrays = {
        "x": np.asarray(L0_attn_x), "wq": by_pair(L0_attn_W_Q), "wk": by_pair(L0_attn_W_K), "wv": by_pair(L0_attn_W_V),
        "wo": np.ascontiguousarray(np.asarray(L0_attn_W_O).transpose(0, 2, 1).reshape(PAIRS, 2 * DH, D)),
        "gate_w": np.asarray(L0_ffn_gate_w), "gate_b": np.asarray(L0_ffn_gate_b),
        "w1": np.asarray(L0_ffn_w1), "b1": np.asarray(L0_ffn_b1), "w2": np.asarray(L0_ffn_w2),
        "b2": np.asarray(L0_ffn_b2),
    }
    nc = bacc.Bacc("TRN2", target_bir_lowering=False, num_devices=1)
    args = [nc.dram_tensor(f"{n}_in", a.shape, mybir.dt.from_np(a.dtype), kind="ExternalInput").ap()
            for n, a in arrays.items()]
    out = nc.dram_tensor("out", [B, S, D], F32, kind="ExternalOutput").ap()
    build(nc, *args, out)
    got = run_bass_kernel_spmd(nc, [{f"{n}_in": a for n, a in arrays.items()}], core_ids=[0])
    return got.results[0]["out"]
```

```python
from contextlib import ExitStack

import concourse.bass as bass
from concourse import mybir

F32 = mybir.dt.float32
F16 = mybir.dt.float16
BF16 = mybir.dt.bfloat16
U32 = mybir.dt.uint32
ALU = mybir.AluOpType
ACT = mybir.ActivationFunctionType
AX_X = mybir.AxisListType.X

P = 128
B, S, D = 2, 1024, 128
HEADS, DH = 16, 64
PAIRS = HEADS // 2
TILES = B * S // P
ROWS = S // P
E, CAP, HID, K = 64, 64, 512, 3
HB = HID // P
EPS = 1e-5
MASKED = 1e10 / 8
SCALE = -1.0 / 8
GRP = 4
W4 = GRP * P
QUARTERS = TILES // GRP
ITEMS = 2 * B * ROWS
MID_FFN, LAST_FFN = 5, 2
LAST = PAIRS - 1
SLOTS = 4
SPLIT_STEP = 19
PROLOGUE_USES = 6
PAST_END = 1 << 20
assert MID_FFN * (PAIRS - 2) + LAST_FFN == E // 2 and LAST_FFN == 2


def row_tile(t):
    return t // (2 * ROWS), (t % (2 * ROWS)) // 2, t % 2


def chunk_plan():
    number, n = {}, 0
    for t in range(ITEMS):
        for c in range(row_tile(t)[1] // GRP + 1):
            number[t, c] = n
            n += 1
    return number


MIDDLE = {
    1: [("rsum", 1, 1)], 2: [("pv", 1, 1)], 4: [("out", 1, 1), ("hidT", 0)], 5: [("q", 1, 0), ("q", 1, 1)],
    7: [("down", 0), ("hidT", 1)], 8: [("tok", 0)], 9: [("tok", 1), ("down", 1), ("hidT", 2)],
    10: [("hidT", 3)], 11: [("k", 1, 0), ("k", 1, 1)], 12: [("down", 2), ("down", 3)],
    13: [("hidT", 4), ("v", 1, 0)], 14: [("rsum", 0, 0), ("up", 0)], 15: [("pv", 0, 0)],
    16: [("out", 0, 0), ("v", 1, 1)], 17: [("rsum", 0, 1)], 19: [("tok", 2), ("up", 1)], 20: [("down", 4)],
    21: [("q", 0, 0), ("q", 0, 1)], 23: [("k", 0, 0), ("pv", 0, 1)], 25: [("tok", 3), ("up", 2), ("out", 0, 1)],
    26: [("rsum", 1, 0), ("k", 0, 1)], 27: [("pv", 1, 0)], 28: [("up", 3)], 29: [("tok", 4), ("v", 0, 0)],
    30: [("up", 4)], 31: [("out", 1, 0), ("v", 0, 1)],
}
FIRST = {
    1: [("v", 1, 0)], 3: [("q", 1, 0), ("q", 1, 1)], 9: [("place", 0), ("k", 1, 0)],
    10: [("place", 1), ("k", 1, 1)], 11: [("v", 1, 1)], 12: [("rsum", 0, 0)], 15: [("pv", 0, 0)],
    21: [("out", 0, 0), ("rsum", 0, 1)], 22: [("q", 0, 0), ("q", 0, 1)], 24: [("k", 0, 0), ("pv", 0, 1)],
    25: [("v", 0, 0)], 26: [("rsum", 1, 0)], 27: [("k", 0, 1)], 28: [("pv", 1, 0)],
    29: [("out", 1, 0), ("out", 0, 1)], 31: [("v", 0, 1)],
}
FINAL = {
    1: [("tok", 5), ("q", 1, 0), ("rsum", 1, 1)], 3: [("tok", 6), ("pv", 1, 1), ("hidT", 0)], 4: [("up", 5)],
    5: [("hidT", 1)], 6: [("down", 0), ("q", 1, 1), ("k", 1, 0)], 7: [("down", 1), ("hidT", 2), ("hidT", 3)],
    8: [("down", 2), ("hidT", 4)], 9: [("out", 1, 1), ("down", 3), ("up", 6)],
    10: [("down", 4), ("hidT", 5), ("hidT", 6)], 11: [("down", 5), ("down", 6), ("k", 1, 1)], 12: [("v", 1, 0)],
    14: [("rsum", 0, 0)], 15: [("pv", 0, 0)], 19: [("rsum", 0, 1)], 21: [("v", 1, 1)], 23: [("pv", 0, 1)],
    25: [("out", 0, 0)], 27: [("rsum", 1, 0)], 30: [("pv", 1, 0)], 31: [("out", 1, 0), ("out", 0, 1)],
}


def misc_plan(kind):
    def has(use):
        left = use[0] in ("rsum", "pv", "out") and use[1:] == (1, 1)
        return {"second": use[0] not in ("hidT", "down"), "end": left}.get(kind, True)

    table = {"first": FIRST, "last": FINAL}.get(kind, MIDDLE)
    steps = {s: [use for use in uses if has(use)] for s, uses in table.items()}
    number = {use: n for n, use in enumerate(use for s in sorted(steps) for use in steps[s])}
    return steps, number


KINDS = ("first", "second", "mid", "last", "end")
CHUNK = chunk_plan()
PLAN = {kind: misc_plan(kind) for kind in KINDS}
CHUNKS = len(CHUNK)
USES = {kind: len(PLAN[kind][1]) for kind in KINDS}
FIRST_MID = 2
MIDS = LAST - FIRST_MID
BEFORE = {"first": PROLOGUE_USES, "second": PROLOGUE_USES + USES["first"]}
BEFORE["mid"] = BEFORE["second"] + USES["second"]
BEFORE["last"] = BEFORE["mid"] + MIDS * USES["mid"]
BEFORE["end"] = BEFORE["last"] + USES["last"]
assert CHUNKS % 2 == USES["mid"] % 2 == 0
GELUS = {"mid": {2: range(MID_FFN)}, "last": {2: range(MID_FFN), 9: (5, 6)}}
ENDING = {("last", 22): [("sum", 0)], ("last", 29): [("sum", 1)],
          ("end", 1): [("sum", 2), ("finish", 0), ("finish", 1)], ("end", 2): [("finish", 2)],
          ("end", 4): [("sum", 3), ("finish", 3)]}
ROUTING = {0: ("argmax 0", "argmax 1"), 1: ("hot 0",), 2: ("hot 1",), 4: ("hot 2",), 6: ("two",), 7: ("chosen",),
           9: ("gates",), 12: ("place 0",), 14: ("place 1", "slots")}
GATE_STEP = 8


def in_bank(n, bank):
    return (n + 1 - bank) // 2


def build(nc, x, wq, wk, wv, wo, gate_w, gate_b, w1, b1, w2, b2, out):
    slots = nc.dram_tensor("slots_dram", [E * CAP, D], F32).ap()
    results = nc.dram_tensor("results_dram", [E * CAP, D], F32).ap()

    x_v = x.rearrange("b (t p) d -> p (b t) d", p=P)
    out_v = out.rearrange("b (t p) d -> p (b t) d", p=P)

    with ExitStack() as ctx:
        def sb(name, shape, dt=F32):
            return ctx.enter_context(nc.sbuf_tensor(name, shape, dt))

        def psum(name, shape, dt=F32):
            return ctx.enter_context(nc.psum_tensor(name, shape, dt))

        def sem(name):
            return ctx.enter_context(nc.semaphore(name))

        ps_s = [psum(f"ps_s{i}", [P, S]) for i in range(2)]
        ps_t = [psum(f"ps_t{i}", [P, W4]) for i in range(2)]
        ps_m = [psum(f"ps_m{i}", [P, W4]) for i in range(2)]

        ident = sb("ident", [P, P])
        ident_b = sb("ident_b", [P, P], BF16)
        mask = sb("mask", [P, P], BF16)
        earlier = sb("earlier", [P, P], BF16)
        ones_b = sb("ones_b", [P, P], BF16)
        iota_e = sb("iota_e", [P, E])
        xn = sb("xn", [P, TILES, D])
        xT_hl = sb("xT_hl", [P, 2, B * S], F16)
        s_acc = sb("s_acc", [P, TILES, D])
        w_qkv = sb("w_qkv", [P, 3, P])
        w_hl = sb("w_hl", [P, 2, 3, P], F16)
        w_o = sb("w_o", [P, D])
        parts = sb("parts", [P, 4, S], F16)
        q_hl = [sb(f"q_hl{b}", [P, 2, S], F16) for b in range(B)]
        k_hh = [sb(f"k_hh{b}", [P, 2, S], F16) for b in range(B)]
        k_ll = [sb(f"k_ll{b}", [P, 2, S], F16) for b in range(B)]
        v_sb = [sb(f"v_sb{b}", [P, ROWS, P]) for b in range(B)]
        probs = sb("probs", [P, SLOTS, S])
        row_min = sb("row_min", [P, 4])
        row_sum = sb("row_sum", [P, B, ROWS, 2, 1])
        row_rec = sb("row_rec", [P, 2, 2 * GRP, 1])
        rec_wide = sb("rec_wide", [P, 2, 2 * GRP, DH])
        probsT = [sb(f"probsT{g}", [P, 2, GRP * (g + 1), W4]) for g in range(2)]
        rec_rows = sb("rec_rows", [P, 2, W4])
        z_sb = sb("z_sb", [P, 2, W4])
        tok = sb("tok", [P, 3, D])
        w1_sb = sb("w1_sb", [P, 3, 2, HID])
        b1_sb = sb("b1_sb", [P, 3, HID])
        w2_sb = sb("w2_sb", [P, MID_FFN, 2, HB, D])
        b2_sb = sb("b2_sb", [P, MID_FFN, D])
        tokT = sb("tokT", [P, 2, P])
        hid = sb("hid", [P, MID_FFN, HID])
        hidT = sb("hidT", [P, 2, HB, P])
        y_sb = sb("y_sb", [P, MID_FFN, D])
        gate_w_sb = sb("gate_w_sb", [P, E])
        gate_b_sb = sb("gate_b_sb", [P, 1, E])
        rstd = sb("rstd", [P, TILES])
        expert = sb("expert", [P, TILES, K, 1])
        place = sb("place", [P, TILES, K])
        over = sb("over", [P, TILES, K])
        gate = sb("gate", [P, TILES, K])
        gate_sum = sb("gate_sum", [P, TILES, 1])
        to_slot = sb("to_slot", [P, TILES * K], U32)
        from_slot = sb("from_slot", [P, TILES * K], U32)
        hid_flat = hid[:, :, :].rearrange("p a b -> p (a b)")
        hot = w1_sb[:, :, :, :].rearrange("p a b c -> p (a b c)").rearrange("p (t k e) -> p t k e", t=TILES, k=K)
        hot_pos = w2_sb[:, 1:4, :, :, :].rearrange("p a b c d -> p (a b c d)").rearrange(
            "p (t k e) -> p t k e", t=TILES, k=K)
        logits = hid_flat[:, 0:TILES * E].rearrange("p (t e) -> p t e", t=TILES)
        two_hot = hid_flat[:, TILES * E:2 * TILES * E].rearrange("p (t e) -> p t e", t=TILES)
        chosen = b1_sb[:, 0, :].bitcast(BF16).rearrange("p (t e) -> p t e", t=TILES)
        top = b1_sb[:, 1, 0:128].rearrange("p (t k) -> p t k", t=TILES)
        top_i = b1_sb[:, 1, 128:256].bitcast(U32).rearrange("p (t k) -> p t k", t=TILES)
        stats = b1_sb[:, 1, 256:352].rearrange("p (t k) -> p t k", t=TILES)
        mean_var = b1_sb[:, 1, 352:384].rearrange("p (t k) -> p t k", t=TILES)
        xnT = probs[:, 0:2, :].rearrange("p a b -> p (a b)")
        zeros = w2_sb[:, 0, :, :, :].rearrange("p a b c -> p (a b c)")
        x_sb = s_acc
        x_late = parts[:, :, :].rearrange("p a s -> p (a s)").bitcast(F32).rearrange("p (t d) -> p t d", t=TILES)
        f_sum = xn
        gathered = [whole.rearrange("p (i k d) -> p i k d", k=K, d=D) for whole in (
            w1_sb[:, :, :, :].rearrange("p a b c -> p (a b c)")[:, 0:GRP * K * D],
            w1_sb[:, :, :, :].rearrange("p a b c -> p (a b c)")[:, GRP * K * D:2 * GRP * K * D],
            b1_sb[:, :, :].rearrange("p a b -> p (a b)"),
            w2_sb[:, :, :, :, :].rearrange("p a b c d -> p (a b c d)")[:, 0:GRP * K * D])]

        x_in = [sem(f"x_in{i}") for i in range(4)]
        gate_in = sem("gate_in")
        var_ready = sem("var_ready")
        std_ready = sem("std_ready")
        xT_ready = sem("xT_ready")
        xT_high = sem("xT_high")
        xT_low = sem("xT_low")
        xT_copied = sem("xT_copied")
        consts = sem("consts")
        acc_zero = sem("acc_zero")
        xn_ready = sem("xn_ready")
        logits_ready = sem("logits_ready")
        logits_read = sem("logits_read")
        chosen_ready = sem("chosen_ready")
        gate_diff = sem("gate_diff")
        gate_exp = sem("gate_exp")
        routed = sem("routed")
        zero_set = sem("zero_set")
        zero_filled = sem("zero_filled")
        scattered = sem("scattered")
        dve_chain = sem("dve_chain")
        pool_chain = sem("pool_chain")

        w_in = sem("w_in")
        w_high = sem("w_high")
        w_split = sem("w_split")
        wo_in = sem("wo_in")
        stacked = [sem(f"stacked{b}") for b in range(B)]
        hi_ready = sem("hi_ready")
        scores_ready = sem("scores_ready")
        min_ready = sem("min_ready")
        exp_ready = sem("exp_ready")
        rec_made = sem("rec_made")
        rec_ready = sem("rec_ready")
        t_ready = sem("t_ready")
        t_done = [sem(f"t_done{i}") for i in range(2)]
        misc_ready = sem("misc_ready")
        misc_done = [sem(f"misc_done{i}") for i in range(2)]
        ffn_in = [sem(f"ffn_in{e}") for e in range(MID_FFN)]
        down_in = [sem(f"down_in{e}") for e in range(MID_FFN)]
        gelu_done = sem("gelu_done")
        y_stored = [sem(f"y_stored{e}") for e in range(MID_FFN)]
        got = [sem(f"got{q}") for q in range(QUARTERS)]
        summed = sem("summed")
        x_again = sem("x_again")
        silu_ready = sem("silu_ready")
        result = sem("result")
        stored = sem("stored")

        def misc(p, kind, use):
            n = BEFORE[kind] + PLAN[kind][1][use]
            if kind != "mid":
                return n % 2, n // 2, n
            return n % 2, n // 2 + (p - FIRST_MID) * (USES["mid"] // 2), n + (p - FIRST_MID) * USES["mid"]

        def uses_before(p, kind, bank=None):
            n, m = (BEFORE[kind], USES["mid"]) if bank is None else (in_bank(BEFORE[kind], bank), USES["mid"] // 2)
            return n if kind != "mid" else n + (p - FIRST_MID) * m

        def wait_misc_ready(eng, p, kind, use):
            eng.wait_ge(misc_ready, misc(p, kind, use)[2] + 1)

        def wait_misc_done(eng, p, kind, use):
            bank, before, _ = misc(p, kind, use)
            eng.wait_ge(misc_done[bank], before + 1)

        def iterations(eng, body):
            body(0, "first")
            body(1, "second")
            with eng.Fori(FIRST_MID, LAST) as p:
                body(p, "mid")
            body(LAST, "last")
            body(PAIRS, "end")

        block = ctx.enter_context(nc.Block())

        @block.sync
        def _(sp):
            def load_x(b):
                for i in (2 * b, 2 * b + 1):
                    sp.dma_start(x_sb[:, 4 * i:4 * i + 4, :], x_v[:, 4 * i:4 * i + 4, :]).then_inc(x_in[i], 16)

            def load_heads(pair):
                for i, w in enumerate((wq, wk, wv)):
                    sp.dma_start(w_qkv[:, i, :], w[pair, :, :]).then_inc(w_in, 16)

            def load_wo(pair):
                sp.dma_start(w_o[:, :], wo[pair, :, :]).then_inc(wo_in, 16)

            def stack(b, what="qk"):
                moves = {"q": ((q_hl, 0, 0), (q_hl, 1, 1)),
                         "k": ((k_hh, 0, 2), (k_hh, 1, 2), (k_ll, 0, 3), (k_ll, 1, 3))}
                for dst, half, i in (move for one in what for move in moves[one]):
                    for h in range(2):
                        sp.dma_start(dst[b][DH * half:DH * half + DH, h, :],
                                     parts[DH * h:DH * h + DH, i, :]).then_inc(stacked[b], 16)

            def load_up(pair, e):
                sp.dma_start(tok[:, e % 3, :], slots[bass.ds(pair * P, P), :]).then_inc(ffn_in[e], 16)
                sp.dma_start(w1_sb[:, e % 3, :, :],
                             w1[bass.ds(pair * 2, 2), :, :].rearrange("e d h -> d e h")).then_inc(ffn_in[e], 16)
                for i in range(2):
                    sp.dma_start(b1_sb[64 * i:64 * i + 64, e % 3, :],
                                 b1[bass.ds(pair * 2 + i, 1), :].to_broadcast([64, HID])).then_inc(ffn_in[e], 16)

            def load_down(pair, e):
                for i in range(2):
                    sp.dma_start(w2_sb[:, e, i, :, :].rearrange("p a b -> p (a b)"),
                                 w2[bass.ds(pair * 2 + i, 1), :, :].rearrange("e (p t) d -> (e p) (t d)", t=HB)
                                 ).then_inc(down_in[e], 16)
                    sp.dma_start(b2_sb[64 * i:64 * i + 64, e, :],
                                 b2[bass.ds(pair * 2 + i, 1), :].to_broadcast([64, D])).then_inc(down_in[e], 16)

            load_x(0)
            load_heads(0)
            load_x(1)
            sp.dma_start(gate_w_sb[:, :], gate_w).then_inc(gate_in, 16)
            sp.dma_start(gate_b_sb[:, 0, :], gate_b.rearrange("(a e) -> a e", a=1).to_broadcast([P, E])
                         ).then_inc(gate_in, 16)
            load_wo(0)
            for n, what in enumerate("qk"):
                for i in range(2):
                    sp.wait_ge(misc_done[i], n + 1)
                stack(0, what)
            sp.wait_ge(zero_set, 1)
            for i in range(4):
                sp.dma_start(slots.rearrange("(q p r) d -> q p (r d)", q=4, p=P)[i, :, :], zeros).then_inc(
                    zero_filled, 16)

            def body(p, kind):
                first_pair = (p - 1) * MID_FFN

                def number(value):
                    return value if isinstance(value, int) else sp.snap(sp.to_reg(value))

                def done(use):
                    return misc_done[misc(p, kind, use)[0]], number(misc(p, kind, use)[1] + 1)

                if kind == "end":
                    return
                scored_before = number(p * ITEMS)
                scored_half = number(p * ITEMS + ITEMS // 2)
                k_done = {(b, i): done(("k", b, i)) for b in ((0, 1) if kind != "last" else (1,)) for i in range(2)}
                own = kind in ("second", "mid")
                left = kind in ("mid", "last")
                up_done = [done(("up", e)) for e in range(MID_FFN)] if own else []
                down_done = [done(("down", e)) for e in range(MID_FFN)] if left else []
                if kind != "first":
                    out_made = number(misc(p, kind, ("out", 1, 1))[2] + 1)
                split = number(p + 1)
                stores = number(16 * (p - 1))

                if kind != "last":
                    sp.wait_ge(w_split, split)
                    load_heads(p + 1)
                if kind == "second":
                    sp.wait_ge(scattered, 16 * TILES * K)
                    load_up(0, 0)
                    load_up(1, 1)
                if own:
                    load_up(first_pair + 2, 2)

                def results_out(e):
                    if left:
                        sp.wait_ge(*down_done[e])
                        store_y(first_pair - MID_FFN + e, e)
                    if own or left and e < LAST_FFN:
                        load_down(first_pair + e, e)

                if kind == "last":
                    for e in range(LAST_FFN):
                        results_out(e)
                if kind != "first":
                    sp.wait_ge(misc_ready, out_made)
                    load_wo(p)
                if kind == "last":
                    for e in range(LAST_FFN, MID_FFN):
                        results_out(e)
                    for e in range(LAST_FFN):
                        sp.wait_ge(*done(("down", MID_FFN + e)))
                        store_y(first_pair + e, e)
                for i in range(2):
                    sp.wait_ge(*k_done[1, i])
                if kind != "first":
                    sp.wait_ge(scores_ready, scored_before)
                stack(1)
                if kind == "last":
                    sp.wait_ge(stacked[1], 192 * (p + 1))
                    sp.dma_start(x_late, x_v).then_inc(x_again, 16)
                    return
                if own:
                    for e in (3, 4):
                        sp.wait_ge(*up_done[e - 3])
                        load_up(first_pair + e, e)
                for e in range(MID_FFN):
                    results_out(e)
                for i in range(2):
                    sp.wait_ge(*k_done[0, i])
                sp.wait_ge(scores_ready, scored_half)
                if kind == "mid":
                    for e in range(MID_FFN):
                        sp.wait_ge(y_stored[e], stores)
                stack(0)
                if own:
                    for e in (0, 1):
                        sp.wait_ge(*up_done[3 + e])
                        load_up(first_pair + MID_FFN + e, e)

            def store_y(pair, e):
                sp.dma_start(results[bass.ds(pair * P, P), :], y_sb[:, e, :]).then_inc(y_stored[e], 16)

            iterations(sp, body)
            for q in range(QUARTERS):
                sp.wait_ge(result, q + 1)
                sp.dma_start(out_v[:, GRP * q:GRP * q + GRP, :], f_sum[:, GRP * q:GRP * q + GRP, :]).then_inc(stored, 16)
            sp.wait_ge(stored, 16 * QUARTERS)

        @block.gpsimd
        def _(pool):
            def link(n, ins):
                ins.then_inc(pool_chain, 1)
                pool.wait_ge(pool_chain, n)

            pool.memset(ident[:, :], 0.0)
            pool.memset(ident_b[:, :], 0.0)
            pool.memset(mask[:, :], MASKED)
            pool.memset(earlier[:, :], 1.0)
            pool.memset(ones_b[:, :], 1.0)
            link(1, pool.memset(iota_e[:, :], 0.0))
            diagonal = dict(compare_op=ALU.not_equal, fill=1.0, base=0, pattern=[[-1, P]], channel_multiplier=1)
            above = dict(compare_op=ALU.is_gt, fill=0.0, base=0, pattern=[[1, P]], channel_multiplier=-1)
            pool.affine_select(out=ident[:, :], in_=ident[:, :], **diagonal)
            pool.affine_select(out=ident_b[:, :], in_=ident_b[:, :], **diagonal)
            pool.affine_select(out=mask[:, :], in_=mask[:, :], **above)
            pool.affine_select(out=earlier[:, :], in_=earlier[:, :], **above)
            pool.iota(iota_e[:, :], pattern=[[1, E]], base=0, channel_multiplier=0,
                      allow_small_or_imprecise_dtypes=True).then_inc(consts, 1)
            pool.memset(zeros, 0.0).then_inc(zero_set, 1)
            pool.wait_ge(xn_ready, TILES)
            pool.memset(s_acc[:, :, :], 0.0).then_inc(acc_zero, 1)
            pool.wait_ge(zero_filled, 64)
            pool.wait_ge(routed, 1)
            for t in range(TILES):
                for k in range(K):
                    n = t * K + k
                    pool.indirect_dma_start(slots, bass.IndirectOffsetOnAxis(ap=to_slot[:, n:n + 1], axis=0),
                                            xn[:, t, :], None, bounds_check=E * CAP - 1,
                                            oob_is_err=False).then_inc(scattered, 16)
            for e in range(MID_FFN):
                pool.wait_ge(y_stored[e], 16 * (PAIRS - 2 + (e < LAST_FFN)))
            for t in range(TILES):
                for k in range(K):
                    n = t * K + k
                    pool.indirect_dma_start(gathered[t // GRP][:, t % GRP, k, :], None, results,
                                            bass.IndirectOffsetOnAxis(ap=from_slot[:, n:n + 1], axis=0),
                                            bounds_check=E * CAP - 1, oob_is_err=False).then_inc(got[t // GRP], 16)

        @block.tensor
        def _(pe):
            pe.wait_ge(consts, 1)

            def transpose_x(b):
                for t in range(ROWS * b, ROWS * b + ROWS):
                    pe.wait_ge(xn_ready, t + 1)
                    pe.transpose(ps_s[b][:, P * (t % ROWS):P * (t % ROWS) + P], xn[:, t, :], ident[:, :]).then_inc(
                        xT_ready, 1)

            def project(b, what, n, bank):
                at = S * b + W4 * n
                x_h, x_l = xT_hl[:, 0, :], xT_hl[:, 1, :]
                w_h, w_l = (w_hl[:, half, "qkv".index(what), :] for half in range(2))
                terms = ((w_h, x_h), (w_h, x_l), (w_l, x_h))
                if what != "v":
                    for m, (w, x) in enumerate(terms):
                        last = pe.matmul(ps_m[bank][:, :], w, x[:, at:at + W4], start=(m == 0), stop=(m == 2))
                    return last
                for i in range(GRP):
                    for m, (w, x) in enumerate(terms):
                        last = pe.matmul(ps_m[bank][:, P * i:P * i + P], x[:, at + P * i:at + P * i + P], w,
                                         start=(m == 0), stop=(m == 2))
                return last

            transpose_x(0)
            pe.wait_ge(w_split, 1)
            for n, (what, i) in enumerate((("q", 0), ("q", 1), ("k", 0), ("k", 1), ("v", 0), ("v", 1))):
                if n < 2:
                    pe.wait_ge(xT_low, n + 1)
                else:
                    pe.wait_ge(misc_done[n % 2], n // 2)
                if (what, i) == ("v", 0):
                    transpose_x(1)
                project(0, what, i, n % 2).then_inc(misc_ready, 1)
            pe.wait_ge(gate_in, 32)
            pe.wait_ge(xT_low, 4)
            pe.wait_ge(xT_copied, 4)
            for t in range(TILES):
                last = pe.matmul(ps_s[0][:, E * t:E * t + E], xnT[:, P * t:P * t + P], gate_w_sb[:, :],
                                 start=True, stop=True)
            last.then_inc(logits_ready, 1)
            pe.wait_ge(logits_read, 1)

            def body(p, kind):
                steps = PLAN[kind][0]

                def scores(t):
                    b, i, h = row_tile(t)
                    if t % (ITEMS // 2) == 0:
                        pe.wait_ge(stacked[b], 192 * (p + 1))
                    if kind != "first" or t >= 2:
                        pe.wait_ge(exp_ready, p * ITEMS + t - 1)
                    rows = slice(P * i, P * i + P)
                    n = P * (i + 1)
                    for c in range(0, n, W4):
                        cols = slice(c, min(c + W4, n))
                        o = ps_s[t % 2][:, cols]
                        has_diagonal = cols.stop == n
                        pe.matmul(o, k_hh[b][:, h, rows], q_hl[b][:, h, cols], start=True, stop=False)
                        last = pe.matmul(o, k_ll[b][:, h, rows], q_hl[b][:, h, cols], start=False,
                                         stop=not has_diagonal)
                    last = pe.matmul(ps_s[t % 2][:, P * i:n], ident_b[:, :], mask[:, :], start=False, stop=True)
                    last.then_inc(scores_ready, 1)

                def transposes(p, t):
                    b, i, h = row_tile(t)
                    pe.wait_ge(exp_ready, p * ITEMS + t + 1)
                    for c in range(i // GRP + 1):
                        n = CHUNK[t, c]
                        if not isinstance(p, int) or p or n >= 2:
                            pe.wait_ge(t_done[n % 2], p * (CHUNKS // 2) + n // 2)
                        for j in range(GRP * c, min(GRP * c + GRP, i + 1)):
                            last = pe.transpose(ps_t[n % 2][:, P * (j % GRP):P * (j % GRP) + P],
                                                probs[:, t % SLOTS, P * j:P * j + P], ident[:, :])
                        last.then_inc(t_ready, 1)

                def misc_use(use):
                    what = use[0]
                    bank, before, _ = misc(p, kind, use)
                    o = ps_m[bank]
                    pe.wait_ge(misc_done[bank], before)
                    if what in "qkv":
                        _, b, i = use
                        pe.wait_ge(w_split, p + 1 if b else p + 2)
                        return project(b, what, i, bank)
                    if what == "place":
                        pe.wait_ge(chosen_ready, 1)
                        for t in range(ROWS * use[1], ROWS * use[1] + ROWS):
                            place_t = o[:, E * (t % ROWS):E * (t % ROWS) + E]
                            last = pe.matmul(place_t, earlier[:, :], chosen[:, t, :], start=True, stop=(t == 0))
                            for u in range(t):
                                last = pe.matmul(place_t, ones_b[:, :], chosen[:, u, :], start=False,
                                                 stop=(u == t - 1))
                        return last
                    if what == "rsum":
                        _, b, g = use
                        pe.wait_ge(rec_ready, 4 * p if b and g else 4 * p + 2 * b + g + 1)
                        for i in range(GRP):
                            last = pe.transpose(
                                o[:, P * i:P * i + P],
                                rec_wide[:, g, 2 * i:2 * i + 2, :].rearrange("p h d -> p (h d)"), ident[:, :])
                        return last
                    if what == "pv":
                        _, b, g = use
                        q = p - 1 if b and g else p
                        last_item = 2 * ROWS * b + 8 * g + 7
                        for m in (CHUNK[last_item, g], CHUNK[last_item, g] - 1):
                            pe.wait_ge(t_done[m % 2], q * (CHUNKS // 2) + m // 2 + 1)
                        for i in range(2):
                            if b == 1 and g == 0:
                                wait_misc_done(pe, p, kind, ("v", 1, i))
                            else:
                                pe.wait_ge(misc_done[i], uses_before(p, kind, i))
                        tiles = GRP * (g + 1)
                        for j in range(tiles):
                            off = P * max(0, j - GRP * g)
                            for h in range(2):
                                last = pe.matmul(o[DH * h:DH * h + DH, off:W4], v_sb[b][:, j, DH * h:DH * h + DH],
                                                 probsT[g][:, h, j, off:W4], start=(j == 0), stop=(j == tiles - 1))
                        return last
                    if what == "out":
                        _, b, g = use
                        wait_misc_done(pe, p, kind, ("pv", b, g))
                        pe.wait_ge(wo_in, 16 * p if b and g else 16 * (p + 1))
                        for i in range(GRP):
                            last = pe.matmul(o[:, P * i:P * i + P], z_sb[:, g, P * i:P * i + P], w_o[:, :],
                                             start=True, stop=True)
                        return last
                    e = use[1]
                    e, own = e % MID_FFN, e
                    if what == "tok":
                        pe.wait_ge(ffn_in[e], 64 * p)
                        return pe.transpose(o[:, 0:P], tok[:, e % 3, :], ident[:, :])
                    if what == "up":
                        wait_misc_done(pe, p, kind, ("tok", own))
                        for i in range(2):
                            last = pe.matmul(o[64 * i:64 * i + 64, :], tokT[:, e % 2, 64 * i:64 * i + 64],
                                             w1_sb[:, e % 3, i, :], start=True, stop=True)
                        return last
                    if what == "hidT":
                        pe.wait_ge(gelu_done, (p - 2) * MID_FFN + own + 1)
                        for j in range(HB):
                            last = pe.transpose(o[:, P * j:P * j + P],
                                                hid[:, e, :].rearrange("p (r t) -> p t r", t=HB)[:, j, :], ident[:, :])
                        return last
                    wait_misc_done(pe, p, kind, ("hidT", own))
                    pe.wait_ge(down_in[e], 64 * (p - 1) if own < MID_FFN else 64 * p)
                    for j in range(HB):
                        for i in range(2):
                            last = pe.matmul(o[64 * i:64 * i + 64, 0:D], hidT[:, own % 2, j, 64 * i:64 * i + 64],
                                             w2_sb[:, e, i, j, :], start=(j == 0), stop=(j == HB - 1))
                    return last

                for s in range(ITEMS):
                    if kind != "end":
                        scores(s)
                    if s < 2 and kind != "first":
                        transposes(p - 1, ITEMS - 2 + s)
                    if s >= 2 and kind != "end":
                        transposes(p, s - 2)
                    for use in steps.get(s, ()):
                        misc_use(use).then_inc(misc_ready, 1)

            iterations(pe, body)

        @block.scalar
        def _(act):
            def deviation(b):
                rows = rstd[:, ROWS * b:ROWS * b + ROWS]
                act.wait_ge(var_ready, b + 1)
                act.activation(rows, rows, ACT.Sqrt).then_inc(std_ready, 1)

            def high_xT(b):
                for i in range(2):
                    act.wait_ge(xT_ready, ROWS * b + GRP * i + GRP)
                    act.activation(xT_hl[:, 0, S * b + W4 * i:S * b + W4 * i + W4], ps_s[b][:, W4 * i:W4 * i + W4],
                                   ACT.Copy).then_inc(xT_high, 1)

            def high_weights(pair):
                act.wait_ge(w_in, 48 * (pair + 1))
                act.activation(w_hl[:, 0, :, :], w_qkv[:, :, :], ACT.Copy).then_inc(w_high, 1)

            deviation(0)
            high_weights(0)
            high_xT(0)

            def high(what, i, bank):
                act.activation(parts[:, 2 * "qk".index(what), W4 * i:W4 * i + W4], ps_m[bank][:, :], ACT.Copy,
                               scale=(1.0 if what == "q" else SCALE)).then_inc(hi_ready, 1)

            def values(b, i, bank):
                act.activation(v_sb[b][:, GRP * i:GRP * i + GRP, :].rearrange("p a b -> p (a b)"), ps_m[bank][:, :],
                               ACT.Copy).then_inc(misc_done[bank], 1)

            for n, (what, i) in enumerate((("q", 0), ("q", 1), ("k", 0), ("k", 1))):
                act.wait_ge(misc_ready, n + 1)
                high(what, i, n % 2)
                if n == 1:
                    deviation(1)
            high_xT(1)
            for i in range(4):
                act.wait_ge(xT_low, i + 1)
                act.activation(xnT[:, W4 * i:W4 * i + W4], ps_s[i // 2][:, W4 * (i % 2):W4 * (i % 2) + W4],
                               ACT.Copy).then_inc(xT_copied, 1)
            for i in range(2):
                act.wait_ge(misc_ready, 5 + i)
                values(0, i, i)

            def body(p, kind):
                steps = PLAN[kind][0]

                def exponentials(t):
                    b, i, h = row_tile(t)
                    n = P * (i + 1)
                    act.wait_ge(min_ready, p * ITEMS + t + 1)
                    if t >= SLOTS:
                        act.wait_ge(t_ready, p * CHUNKS + CHUNK[t - SLOTS, row_tile(t - SLOTS)[1] // GRP] + 1)
                    elif kind != "first":
                        u = ITEMS + t - SLOTS
                        act.wait_ge(t_ready, (p - 1) * CHUNKS + CHUNK[u, 1] + 1)
                    act.activation(probs[:, t % SLOTS, 0:n], ps_s[t % 2][:, 0:n], ACT.Exp,
                                   bias=row_min[:, t % 4:t % 4 + 1], scale=-1.0,
                                   accum_out=row_sum[:, b, i, h, :]).then_inc(exp_ready, 1)

                def chunk(p, t):
                    b, i, h = row_tile(t)
                    g = i // GRP
                    n = CHUNK[t, g]
                    if i % GRP == 0 and h == 0:
                        if b == 1:
                            wait_misc_ready(act, p, kind, ("pv", 0, g))
                        elif kind != "first":
                            if g == 1:
                                wait_misc_ready(act, p, kind, ("pv", 1, 1))
                            else:
                                act.wait_ge(misc_ready, uses_before(p, kind))
                    act.wait_ge(t_ready, p * CHUNKS + n + 1)
                    m = i % GRP + 1
                    act.activation(probsT[g][:, h, GRP * g:i + 1, P * (i % GRP):P * (i % GRP) + P],
                                   ps_t[n % 2][:, 0:P * m].rearrange("p (a b) -> p a b", b=P),
                                   ACT.Copy).then_inc(t_done[n % 2], 1)

                def widen(p, b, g):
                    act.wait_ge(rec_made, 4 * p + 2 * b + g + 1)
                    act.activation(rec_wide[:, g, :, :], row_rec[:, g, :, :].to_broadcast([P, 2 * GRP, DH]),
                                   ACT.Copy).then_inc(rec_ready, 1)

                def consume(use):
                    what = use[0]
                    bank = misc(p, kind, use)[0]
                    if what in "qk":
                        _, b, i = use
                        if what == "q" and i == 0:
                            act.wait_ge(stacked[1 - b], 192 * (p + 1))
                        wait_misc_ready(act, p, kind, use)
                        high(what, i, bank)
                    elif what == "v":
                        _, b, i = use
                        if b == 0 or kind != "first":
                            wait_misc_ready(act, p, kind, ("pv", b, 1))
                        wait_misc_ready(act, p, kind, use)
                        values(b, i, bank)
                    elif what == "rsum":
                        _, b, g = use
                        if (b, g) == (1, 0):
                            wait_misc_done(act, p, kind, ("pv", 0, 0))
                        elif (b, g) == (0, 1) and kind != "first":
                            wait_misc_done(act, p, kind, ("pv", 1, 1))
                        elif kind != "first":
                            for i in range(2):
                                act.wait_ge(misc_done[i], uses_before(p, kind, i))
                        wait_misc_ready(act, p, kind, use)
                        act.activation(rec_rows[:, g, :], ps_m[bank][:, :], ACT.Copy).then_inc(misc_done[bank], 1)
                    elif what == "hidT":
                        e = use[1]
                        if e >= 2:
                            wait_misc_ready(act, p, kind, ("down", e - 2))
                        wait_misc_ready(act, p, kind, use)
                        act.activation(hidT[:, e % 2, :, :].rearrange("p a b -> p (a b)"), ps_m[bank][:, :],
                                       ACT.Copy).then_inc(misc_done[bank], 1)

                for s in range(ITEMS):
                    if kind != "end":
                        exponentials(s)
                    if s < 2 and kind != "first":
                        chunk(p - 1, ITEMS - 2 + s)
                    if s >= 2 and kind != "end":
                        chunk(p, s - 2)
                    if s == 0 and kind != "first":
                        widen(p - 1, 1, 1)
                    if s == GATE_STEP and kind == "first":
                        act.wait_ge(gate_diff, 1)
                        act.activation(gate[:, :, :], gate[:, :, :], ACT.Exp).then_inc(gate_exp, 1)
                    if s and s % 8 == 0 and kind != "end":
                        widen(p, (s - 8) // 16, (s - 8) // 8 % 2)
                    for e in GELUS.get(kind, {}).get(s, ()):
                        if e < MID_FFN:
                            for i in range(2):
                                act.wait_ge(misc_done[i], uses_before(p, kind, i))
                        else:
                            wait_misc_done(act, p, kind, ("up", e))
                        x_e = hid[:, e % MID_FFN, :]
                        act.activation(x_e, x_e, ACT.Gelu).then_inc(gelu_done, 1)
                    for use in steps.get(s, ()):
                        consume(use)
                    if s == SPLIT_STEP and kind not in ("last", "end"):
                        wait_misc_ready(act, p, kind, ("v", 1, 1))
                        high_weights(p + 1)

            iterations(act, body)
            for q in range(QUARTERS):
                act.wait_ge(summed, q + 1)
                act.activation(f_sum[:, GRP * q:GRP * q + GRP, :], f_sum[:, GRP * q:GRP * q + GRP, :],
                               ACT.Silu).then_inc(silu_ready, 1)

        @block.vector
        def _(dve):
            chain = [0]

            def link(ins):
                chain[0] += 1
                ins.then_inc(dve_chain, 1)
                dve.wait_ge(dve_chain, chain[0])

            def statistics(b):
                tiles = range(ROWS * b, ROWS * b + ROWS)
                for t in tiles:
                    if t % 4 == 0:
                        dve.wait_ge(x_in[t // 4], 16)
                    last = dve.bn_stats(stats[:, t, :], x_sb[:, t, :])
                link(last)
                for t in tiles:
                    last = dve.bn_aggr(mean_var[:, t, :], stats[:, t, :])
                link(last)
                dve.tensor_scalar(rstd[:, tiles.start:tiles.stop], mean_var[:, tiles.start:tiles.stop, 1], EPS, None,
                                  ALU.add).then_inc(var_ready, 1)

            def normalise(b):
                tiles = range(ROWS * b, ROWS * b + ROWS)
                dve.wait_ge(std_ready, b + 1)
                link(dve.reciprocal(rstd[:, tiles.start:tiles.stop], rstd[:, tiles.start:tiles.stop]))
                for t in tiles:
                    dve.tensor_scalar(xn[:, t, :], x_sb[:, t, :], mean_var[:, t, 0:1], rstd[:, t:t + 1],
                                      ALU.subtract, ALU.mult).then_inc(xn_ready, 1)

            def low(what, i, bank):
                q = 2 * "qk".index(what)
                cols = slice(W4 * i, W4 * i + W4)
                dve.scalar_tensor_tensor(out=parts[:, q + 1, cols], in0=ps_m[bank][:, :],
                                         scalar=(1.0 if what == "q" else SCALE), in1=parts[:, q, cols],
                                         op0=ALU.mult, op1=ALU.subtract).then_inc(misc_done[bank], 1)

            def low_weights(pair):
                dve.wait_ge(w_high, pair + 1)
                dve.tensor_tensor(w_hl[:, 1, :, :], w_qkv[:, :, :], w_hl[:, 0, :, :], ALU.subtract).then_inc(w_split, 1)

            def low_xT(b):
                for i in range(2):
                    dve.wait_ge(xT_high, 2 * b + i + 1)
                    cols = slice(S * b + W4 * i, S * b + W4 * i + W4)
                    dve.tensor_tensor(xT_hl[:, 1, cols], ps_s[b][:, W4 * i:W4 * i + W4], xT_hl[:, 0, cols],
                                      ALU.subtract).then_inc(xT_low, 1)

            statistics(0)
            normalise(0)
            low_weights(0)
            low_xT(0)
            statistics(1)
            for n, (what, i) in enumerate((("q", 0), ("q", 1), ("k", 0), ("k", 1))):
                if n == 2:
                    normalise(1)
                dve.wait_ge(hi_ready, n + 1)
                low(what, i, n % 2)

            low_xT(1)
            dve.wait_ge(logits_ready, 1)
            ins = dve.tensor_tensor(logits, ps_s[0][:, :].rearrange("p (t e) -> p t e", t=TILES),
                                    gate_b_sb[:, :, :].to_broadcast([P, TILES, E]), ALU.add)
            ins.then_inc(logits_read, 1)
            dve.wait_ge(logits_read, 1)
            for t in range(TILES):
                last = dve.max(top[:, t, :], logits[:, t, :])
            link(last)

            def route(piece):
                what, n = (piece.split() + ["0"])[:2]
                n = int(n)
                half = slice(ROWS * n, ROWS * n + ROWS)
                if what == "argmax":
                    for t in range(ROWS * n, ROWS * n + ROWS):
                        last = dve.max_index(top_i[:, t, :], top[:, t, :], logits[:, t, :])
                    if n == 1:
                        link(last)
                        link(dve.tensor_copy(expert[:, :, :, 0], top_i[:, :, 0:K]))
                elif what == "hot":
                    last = dve.tensor_tensor(hot[:, :, n, :], expert[:, :, n, :].to_broadcast([P, TILES, E]),
                                             iota_e[:, :].unsqueeze(1).to_broadcast([P, TILES, E]), ALU.is_equal)
                    if n == K - 1:
                        link(last)
                elif what == "two":
                    link(dve.tensor_tensor(two_hot, hot[:, :, 0, :], hot[:, :, 1, :], ALU.add))
                elif what == "chosen":
                    dve.tensor_tensor(chosen[:, :, :], two_hot, hot[:, :, 2, :], ALU.add).then_inc(chosen_ready, 1)
                    dve.tensor_tensor(gate[:, :, :], top[:, :, 0:K], top[:, :, 0:1].to_broadcast([P, TILES, K]),
                                      ALU.subtract).then_inc(gate_diff, 1)
                elif what == "gates":
                    dve.wait_ge(gate_exp, 1)
                    link(dve.tensor_reduce(gate_sum[:, :, 0], gate[:, :, :], AX_X, ALU.add))
                    link(dve.reciprocal(gate_sum[:, :, 0], gate_sum[:, :, 0]))
                    link(dve.tensor_tensor(gate[:, :, :], gate[:, :, :],
                                           gate_sum[:, :, :].to_broadcast([P, TILES, K]), ALU.mult))
                elif what == "place":
                    wait_misc_done(dve, 0, "first", ("place", n))
                    last = dve.tensor_reduce(place[:, half, :], hot_pos[:, half, :, :], AX_X, ALU.add)
                    if n == 1:
                        link(last)
                elif what == "slots":
                    link(dve.tensor_scalar(over[:, :, :], place[:, :, :], float(CAP), None, ALU.is_ge))
                    kept = hot_pos[:, 0, 0, 0:TILES * K].rearrange("p (t k) -> p t k", k=K)
                    slot = hot_pos[:, 1, 0, 0:TILES * K].rearrange("p (t k) -> p t k", k=K)
                    dve.tensor_scalar(kept, over[:, :, :], -1.0, 1.0, ALU.mult, ALU.add)
                    link(dve.scalar_tensor_tensor(out=slot, in0=expert[:, :, :, 0], scalar=float(CAP),
                                                  in1=place[:, :, :], op0=ALU.mult, op1=ALU.add))
                    dve.scalar_tensor_tensor(out=to_slot[:, :].rearrange("p (t k) -> p t k", k=K),
                                             in0=over[:, :, :], scalar=float(PAST_END), in1=slot, op0=ALU.mult,
                                             op1=ALU.add).then_inc(routed, 1)
                    dve.tensor_tensor(gate[:, :, :], gate[:, :, :], kept, ALU.mult)
                    link(dve.tensor_scalar(place[:, :, :], place[:, :, :], float(CAP - 1), None, ALU.min))
                    link(dve.scalar_tensor_tensor(out=from_slot[:, :].rearrange("p (t k) -> p t k", k=K),
                                                  in0=expert[:, :, :, 0], scalar=float(CAP), in1=place[:, :, :],
                                                  op0=ALU.mult, op1=ALU.add))

            def gather_sum(q):
                dve.wait_ge(got[q], 16 * K * GRP)
                for k in range(K):
                    for i in range(GRP):
                        t = GRP * q + i
                        if k == 0:
                            last = dve.tensor_scalar(f_sum[:, t, :], gathered[q][:, i, k, :], gate[:, t, k:k + 1],
                                                     None, ALU.mult)
                        else:
                            last = dve.scalar_tensor_tensor(out=f_sum[:, t, :], in0=gathered[q][:, i, k, :],
                                                            scalar=gate[:, t, k:k + 1], in1=f_sum[:, t, :],
                                                            op0=ALU.mult, op1=ALU.add)
                    if k == K - 1:
                        last.then_inc(summed, 1)
                    else:
                        link(last)

            def finish(q):
                tiles = slice(GRP * q, GRP * q + GRP)
                dve.wait_ge(silu_ready, q + 1)
                kind, p = ("end", PAIRS) if q == QUARTERS - 1 else ("last", LAST)
                wait_misc_done(dve, p, kind, ("out", q // 2, q % 2))
                link(dve.tensor_tensor(f_sum[:, tiles, :], f_sum[:, tiles, :], s_acc[:, tiles, :], ALU.mult))
                if q == 0:
                    dve.wait_ge(x_again, 16)
                dve.tensor_tensor(f_sum[:, tiles, :], f_sum[:, tiles, :], x_late[:, tiles, :], ALU.add).then_inc(
                    result, 1)

            def body(p, kind):
                steps = PLAN[kind][0]

                def minima(t):
                    b, i, h = row_tile(t)
                    dve.wait_ge(scores_ready, p * ITEMS + t + 1)
                    dve.tensor_reduce(row_min[:, t % 4:t % 4 + 1], ps_s[t % 2][:, 0:P * (i + 1)], AX_X,
                                      ALU.min).then_inc(min_ready, 1)

                def first_chunk(p, t):
                    b, i, h = row_tile(t)
                    if i < GRP:
                        return
                    n = CHUNK[t, 0]
                    if i == GRP and h == 0:
                        if b == 1:
                            wait_misc_ready(dve, p, kind, ("pv", 0, 1))
                        elif kind != "first":
                            wait_misc_ready(dve, p, kind, ("pv", 1, 1))
                    dve.wait_ge(t_ready, p * CHUNKS + n + 1)
                    dve.tensor_copy(probsT[1][:, h, 0:GRP, P * (i % GRP):P * (i % GRP) + P],
                                    ps_t[n % 2][:, :].rearrange("p (a b) -> p a b", b=P)).then_inc(t_done[n % 2], 1)

                def reciprocals(p, b, g):
                    dve.wait_ge(exp_ready, p * ITEMS + 2 * ROWS * b + 8 * g + 8)
                    rows = slice(GRP * g, GRP * g + GRP)
                    dve.reciprocal(row_rec[:, g, :, 0], row_sum[:, b, rows, :, 0].rearrange("p i h -> p (i h)")
                                   ).then_inc(rec_made, 1)

                def consume(use):
                    what = use[0]
                    bank = misc(p, kind, use)[0]
                    if what in "qk":
                        _, b, i = use
                        unit = 2 * p + 1 if b else 2 * p + 2
                        dve.wait_ge(hi_ready, 4 * unit + 2 * "qk".index(what) + i + 1)
                        low(what, i, bank)
                    elif what == "place":
                        half = slice(ROWS * use[1], ROWS * use[1] + ROWS)
                        wait_misc_ready(dve, p, kind, use)
                        for k in range(K):
                            last = dve.tensor_tensor(hot_pos[:, half, k, :],
                                                     ps_m[bank][:, :].rearrange("p (t e) -> p t e", e=E),
                                                     hot[:, half, k, :], ALU.mult)
                        last.then_inc(misc_done[bank], 1)
                    elif what == "pv":
                        _, b, g = use
                        wait_misc_done(dve, p, kind, ("rsum", b, g))
                        wait_misc_ready(dve, p, kind, use)
                        dve.tensor_tensor(z_sb[:, g, :], ps_m[bank][:, :], rec_rows[:, g, :], ALU.mult).then_inc(
                            misc_done[bank], 1)
                    elif what == "out":
                        _, b, g = use
                        wait_misc_ready(dve, p, kind, use)
                        t = ROWS * b + GRP * g
                        acc = s_acc[:, t:t + GRP, :].rearrange("p a b -> p (a b)")
                        if kind == "first":
                            dve.wait_ge(acc_zero, 1)
                        dve.tensor_tensor(acc, ps_m[bank][:, :], acc, ALU.add).then_inc(misc_done[bank], 1)
                    elif what == "tok":
                        e = use[1] % MID_FFN
                        wait_misc_ready(dve, p, kind, use)
                        dve.tensor_copy(tokT[:, e % 2, :], ps_m[bank][:, 0:P]).then_inc(misc_done[bank], 1)
                    elif what == "up":
                        e = use[1] % MID_FFN
                        wait_misc_ready(dve, p, kind, use)
                        dve.tensor_tensor(hid[:, e, :], ps_m[bank][:, :], b1_sb[:, e % 3, :], ALU.add).then_inc(
                            misc_done[bank], 1)
                    elif what == "down":
                        e = use[1] % MID_FFN
                        if use[1] >= MID_FFN:
                            dve.wait_ge(y_stored[e], 16 * (PAIRS - 2))
                        wait_misc_ready(dve, p, kind, use)
                        dve.tensor_tensor(y_sb[:, e, :], ps_m[bank][:, 0:D], b2_sb[:, e, :], ALU.add).then_inc(
                            misc_done[bank], 1)

                for s in range(ITEMS):
                    if kind != "end":
                        minima(s)
                    if s < 2 and kind != "first":
                        first_chunk(p - 1, ITEMS - 2 + s)
                    if s >= 2 and kind != "end":
                        first_chunk(p, s - 2)
                    if s == 0 and kind != "first":
                        reciprocals(p - 1, 1, 1)
                    if s and s % 8 == 0 and kind != "end":
                        reciprocals(p, (s - 8) // 16, (s - 8) // 8 % 2)
                    for use in steps.get(s, ()):
                        consume(use)
                    if s == SPLIT_STEP and kind not in ("last", "end"):
                        low_weights(p + 1)
                    for piece in ROUTING.get(s, ()) if kind == "first" else ():
                        route(piece)
                    for what, q in ENDING.get((kind, s), ()):
                        (gather_sum if what == "sum" else finish)(q)

            iterations(dve, body)


def kernel(L0_attn_x, L0_attn_W_Q, L0_attn_W_K, L0_attn_W_V, L0_attn_W_O, L0_ffn_gate_w, L0_ffn_gate_b, L0_ffn_w1,
           L0_ffn_b1, L0_ffn_w2, L0_ffn_b2):
    import numpy as np
    import concourse.bacc as bacc
    from concourse.bass_utils import run_bass_kernel_spmd

    def by_pair(w):
        return np.ascontiguousarray(np.asarray(w).reshape(PAIRS, 2 * DH, D).transpose(0, 2, 1))

    arrays = {
        "x": np.asarray(L0_attn_x), "wq": by_pair(L0_attn_W_Q), "wk": by_pair(L0_attn_W_K), "wv": by_pair(L0_attn_W_V),
        "wo": np.ascontiguousarray(np.asarray(L0_attn_W_O).transpose(0, 2, 1).reshape(PAIRS, 2 * DH, D)),
        "gate_w": np.asarray(L0_ffn_gate_w), "gate_b": np.asarray(L0_ffn_gate_b),
        "w1": np.asarray(L0_ffn_w1), "b1": np.asarray(L0_ffn_b1), "w2": np.asarray(L0_ffn_w2),
        "b2": np.asarray(L0_ffn_b2),
    }
    nc = bacc.Bacc("TRN2", target_bir_lowering=False, num_devices=1)
    args = [nc.dram_tensor(f"{n}_in", a.shape, mybir.dt.from_np(a.dtype), kind="ExternalInput").ap()
            for n, a in arrays.items()]
    out = nc.dram_tensor("out", [B, S, D], F32, kind="ExternalOutput").ap()
    build(nc, *args, out)
    got = run_bass_kernel_spmd(nc, [{f"{n}_in": a for n, a in arrays.items()}], core_ids=[0])
    return got.results[0]["out"]
```
